# Optimizing a Trainium2 kernel written in Bass

```python
import numpy as np
import jax
import jax.numpy as jnp

def _softmax(x, axis=-1):
    return jax.nn.softmax(x, axis=axis)

def _gelu(x):
    return jax.nn.gelu(x, approximate=True)

def _silu(x):
    return jax.nn.silu(x)

def _sigmoid(x):
    return jax.nn.sigmoid(x)

def _layernorm(x, axis=-1, eps=1e-05):
    m = jnp.mean(x, axis=axis, keepdims=True)
    v = jnp.var(x, axis=axis, keepdims=True)
    return (x - m) / jnp.sqrt(v + eps)

def _scatter_add(tgt, idx, src, axis=0):
    return tgt.at[idx].add(src)

def _segment_sum(src, seg, n):
    return jax.ops.segment_sum(src, seg, n)
kernel_name = 'mk_decoder_postln_d1_seqx_r8_1fe567'

def setup_inputs(seed: int=0):
    np.random.seed(seed)
    _w = jnp.asarray

    def _rec_inputs():
        import jax
        import jax.numpy as jnp
        _rk = jax.random.key(seed)
        x = -0.0002928 + 1 * jax.random.normal(jax.random.fold_in(_rk, 1), (32, 128, 128), jnp.float32)
        _lenS = 128 - jax.random.randint(jax.random.fold_in(_rk, 7), (32,), 0, max(1, 128 // 4) + 1, jnp.int32)
        _lenS2 = 128 - jax.random.randint(jax.random.fold_in(_rk, 8), (32,), 0, max(1, 128 // 4) + 1, jnp.int32)
        _ctx_1024P = jax.random.normal(jax.random.fold_in(_rk, 11), (32, 16, 128), jnp.float32)
        _ctx_1024c = jax.random.dirichlet(jax.random.fold_in(_rk, 511), 0.3 * jnp.ones((16,), jnp.float32), (32, 128))
        _ctx_1024t = jnp.einsum('bsk,bkd->bsd', _ctx_1024c, _ctx_1024P)
        _ctx_1024t = _ctx_1024t * jax.lax.rsqrt(jnp.mean(jnp.square(_ctx_1024t)) + 1e-12) * 0.953939
        ctx_1024 = -1.39393e-06 + 0.999914 * (_ctx_1024t + 0.3 * jax.random.normal(jax.random.fold_in(_rk, 611), (32, 128, 128), jnp.float32))
        fside_BxS2_0 = -0.00600047 + 0.990131 * jax.random.normal(jax.random.fold_in(_rk, 12), (32, 128), jnp.float32)
        return (x, ctx_1024, fside_BxS2_0)
    x, ctx_1024, fside_BxS2_0 = _rec_inputs()

    def _L0_attn_setup():
        import jax, jax.numpy as jnp
        import numpy as np
        from jax import lax
        L, B, T, C, F = (4, 4, 256, 128, 512)
        EPS = 1e-05

        def layernorm(x, w, b):
            m = jnp.mean(x, axis=-1, keepdims=True)
            v = jnp.var(x, axis=-1, keepdims=True)
            return (x - m) * lax.rsqrt(v + EPS) * w + b

        def time_shift(x):
            return jnp.pad(x, ((0, 0), (1, 0), (0, 0)))[:, :-1]

        def wkv(time_decay, time_first, k, v):
            w = -jnp.exp(time_decay)
            u = time_first
            kt = jnp.swapaxes(k, 0, 1)
            vt = jnp.swapaxes(v, 0, 1)
            Bn, Cn = (k.shape[0], k.shape[2])
            init = (jnp.zeros((Bn, Cn), k.dtype), jnp.zeros((Bn, Cn), k.dtype), jnp.full((Bn, Cn), -1e+38, k.dtype))

            def step(carry, kv):
                aa, bb, pp = carry
                kk, vv = kv
                ww = u + kk
                qq = jnp.maximum(pp, ww)
                e1 = jnp.exp(pp - qq)
                e2 = jnp.exp(ww - qq)
                out = (e1 * aa + e2 * vv) / (e1 * bb + e2)
                ww2 = pp + w
                qq2 = jnp.maximum(ww2, kk)
                e1b = jnp.exp(ww2 - qq2)
                e2b = jnp.exp(kk - qq2)
                return ((e1b * aa + e2b * vv, e1b * bb + e2b, qq2), out)
            _, out = lax.scan(step, init, (kt, vt))
            return jnp.swapaxes(out, 0, 1)
        key = jax.random.key(seed)
        ks = jax.random.split(key, 16)
        s = 0.02
        d = {}
        d['x'] = jax.random.normal(ks[0], (B, T, C), jnp.float32)
        d['ln0_w'] = jnp.ones((C,), jnp.float32)
        d['ln0_b'] = jnp.zeros((C,), jnp.float32)
        d['ln1_w'] = jnp.ones((L, C), jnp.float32)
        d['ln1_b'] = jnp.zeros((L, C), jnp.float32)
        d['ln2_w'] = jnp.ones((L, C), jnp.float32)
        d['ln2_b'] = jnp.zeros((L, C), jnp.float32)
        d['time_decay'] = jax.random.normal(ks[1], (L, C), jnp.float32) * 0.5
        d['time_first'] = jax.random.normal(ks[2], (L, C), jnp.float32) * 0.5 + jnp.float32(np.log(0.3))
        d['tmk'] = jax.random.uniform(ks[3], (L, C), jnp.float32)
        d['tmv'] = jax.random.uniform(ks[4], (L, C), jnp.float32)
        d['tmr'] = jax.random.uniform(ks[5], (L, C), jnp.float32)
        d['Wk'] = jax.random.normal(ks[6], (L, C, C), jnp.float32) * s
        d['Wv'] = jax.random.normal(ks[7], (L, C, C), jnp.float32) * s
        d['Wr'] = jax.random.normal(ks[8], (L, C, C), jnp.float32) * s
        d['Wo'] = jax.random.normal(ks[9], (L, C, C), jnp.float32) * s
        d['cmk'] = jax.random.uniform(ks[10], (L, C), jnp.float32)
        d['cmr'] = jax.random.uniform(ks[11], (L, C), jnp.float32)
        d['Wck'] = jax.random.normal(ks[12], (L, F, C), jnp.float32) * s
        d['Wcv'] = jax.random.normal(ks[13], (L, C, F), jnp.float32) * s
        d['Wcr'] = jax.random.normal(ks[14], (L, C, C), jnp.float32) * s
        return d
    _L0_attn_all = _L0_attn_setup()
    _L0_attn_in = {k: v for k, v in _L0_attn_all.items() if k in ('ln0_w', 'ln0_b', 'ln1_w', 'ln1_b', 'ln2_w', 'ln2_b', 'time_decay', 'time_first', 'tmk', 'tmv', 'tmr', 'Wk', 'Wv', 'Wr', 'Wo', 'cmk', 'cmr', 'Wck', 'Wcv', 'Wcr')}
    del _L0_attn_all

    def _L0_xattn_setup():
        import jax, jax.numpy as jnp
        import numpy as np
        EMBED = 128
        NHEAD = 16
        HEAD_DIM = EMBED // NHEAD
        key = jax.random.key(seed)
        ks = jax.random.split(key, 8)
        B, SQ, SKV = (2, 256, 256)
        scale = 1.0 / np.sqrt(EMBED)
        return {'query': jax.random.normal(ks[0], (B, SQ, EMBED), dtype=jnp.float32), 'key': jax.random.normal(ks[1], (B, SKV, EMBED), dtype=jnp.float32), 'value': jax.random.normal(ks[2], (B, SKV, EMBED), dtype=jnp.float32), 'attention_bias': jax.random.normal(ks[3], (B, SKV), dtype=jnp.float32), 'Wq': jax.random.normal(ks[4], (EMBED, EMBED), dtype=jnp.float32) * scale, 'Wk': jax.random.normal(ks[5], (EMBED, EMBED), dtype=jnp.float32) * scale, 'Wv': jax.random.normal(ks[6], (EMBED, EMBED), dtype=jnp.float32) * scale, 'Wo': jax.random.normal(ks[7], (EMBED, EMBED), dtype=jnp.float32) * scale}
    _L0_xattn_all = _L0_xattn_setup()
    _L0_xattn_in = {k: v for k, v in _L0_xattn_all.items() if k in ('Wq', 'Wk', 'Wv', 'Wo')}
    del _L0_xattn_all

    def _L0_ffn_setup():
        import jax, jax.numpy as jnp
        import numpy as np
        H, I, E, NS, C = (128, 128, 6, 2, 2)
        TOPK = 2
        TEMP = 1.0
        EPS = 1e-06
        key = jax.random.key(seed)
        ks = jax.random.split(key, 20)
        sd = 0.02
        inp = {'x': jax.random.normal(ks[0], (4, 256, H), jnp.float32), 'router_W': jax.random.normal(ks[1], (C, H, E), jnp.float32) * sd, 'router_b': jax.random.normal(ks[2], (C, E), jnp.float32) * sd, 'gate_bias': jax.random.normal(ks[3], (C, E), jnp.float32) * sd, 'exp_Wup': jax.random.normal(ks[4], (E, H, I), jnp.float32) * sd, 'exp_bup': jnp.zeros((E, I), jnp.float32), 'exp_Wg': jax.random.normal(ks[5], (E, I, I), jnp.float32) * sd, 'exp_bg': jnp.zeros((E, I), jnp.float32), 'exp_Wdown': jax.random.normal(ks[6], (E, I, H), jnp.float32) * sd, 'exp_bdown': jnp.zeros((E, H), jnp.float32), 'share_Wup': jax.random.normal(ks[7], (H, NS * I), jnp.float32) * sd, 'share_bup': jnp.zeros((NS * I,), jnp.float32), 'share_Wg': jax.random.normal(ks[8], (I, I), jnp.float32) * sd, 'share_bg': jnp.zeros((I,), jnp.float32), 'share_Wdown': jax.random.normal(ks[9], (I, H), jnp.float32) * sd, 'share_bdown': jnp.zeros((H,), jnp.float32), 'norm_w': jnp.ones((C, H), jnp.float32)}
        return inp
    _L0_ffn_all = _L0_ffn_setup()
    _L0_ffn_in = {k: v for k, v in _L0_ffn_all.items() if k in ('router_W', 'router_b', 'gate_bias', 'exp_Wup', 'exp_bup', 'exp_Wg', 'exp_bg', 'exp_Wdown', 'exp_bdown', 'share_Wup', 'share_bup', 'share_Wg', 'share_bg', 'share_Wdown', 'share_bdown', 'norm_w')}
    del _L0_ffn_all
    return {'x': x, 'ctx_1024': ctx_1024, 'fside_BxS2_0': fside_BxS2_0, 'L0_attn_ln0_w': _L0_attn_in['ln0_w'], 'L0_attn_ln0_b': _L0_attn_in['ln0_b'], 'L0_attn_ln1_w': _L0_attn_in['ln1_w'], 'L0_attn_ln1_b': _L0_attn_in['ln1_b'], 'L0_attn_ln2_w': _L0_attn_in['ln2_w'], 'L0_attn_ln2_b': _L0_attn_in['ln2_b'], 'L0_attn_time_decay': _L0_attn_in['time_decay'], 'L0_attn_time_first': _L0_attn_in['time_first'], 'L0_attn_tmk': _L0_attn_in['tmk'], 'L0_attn_tmv': _L0_attn_in['tmv'], 'L0_attn_tmr': _L0_attn_in['tmr'], 'L0_attn_Wk': _L0_attn_in['Wk'], 'L0_attn_Wv': _L0_attn_in['Wv'], 'L0_attn_Wr': _L0_attn_in['Wr'], 'L0_attn_Wo': _L0_attn_in['Wo'], 'L0_attn_cmk': _L0_attn_in['cmk'], 'L0_attn_cmr': _L0_attn_in['cmr'], 'L0_attn_Wck': _L0_attn_in['Wck'], 'L0_attn_Wcv': _L0_attn_in['Wcv'], 'L0_attn_Wcr': _L0_attn_in['Wcr'], 'L0_xattn_Wq': _L0_xattn_in['Wq'], 'L0_xattn_Wk': _L0_xattn_in['Wk'], 'L0_xattn_Wv': _L0_xattn_in['Wv'], 'L0_xattn_Wo': _L0_xattn_in['Wo'], 'L0_ffn_router_W': _L0_ffn_in['router_W'], 'L0_ffn_router_b': _L0_ffn_in['router_b'], 'L0_ffn_gate_bias': _L0_ffn_in['gate_bias'], 'L0_ffn_exp_Wup': _L0_ffn_in['exp_Wup'], 'L0_ffn_exp_bup': _L0_ffn_in['exp_bup'], 'L0_ffn_exp_Wg': _L0_ffn_in['exp_Wg'], 'L0_ffn_exp_bg': _L0_ffn_in['exp_bg'], 'L0_ffn_exp_Wdown': _L0_ffn_in['exp_Wdown'], 'L0_ffn_exp_bdown': _L0_ffn_in['exp_bdown'], 'L0_ffn_share_Wup': _L0_ffn_in['share_Wup'], 'L0_ffn_share_bup': _L0_ffn_in['share_bup'], 'L0_ffn_share_Wg': _L0_ffn_in['share_Wg'], 'L0_ffn_share_bg': _L0_ffn_in['share_bg'], 'L0_ffn_share_Wdown': _L0_ffn_in['share_Wdown'], 'L0_ffn_share_bdown': _L0_ffn_in['share_bdown'], 'L0_ffn_norm_w': _L0_ffn_in['norm_w']}

def reference(x, ctx_1024, fside_BxS2_0, L0_attn_ln0_w, L0_attn_ln0_b, L0_attn_ln1_w, L0_attn_ln1_b, L0_attn_ln2_w, L0_attn_ln2_b, L0_attn_time_decay, L0_attn_time_first, L0_attn_tmk, L0_attn_tmv, L0_attn_tmr, L0_attn_Wk, L0_attn_Wv, L0_attn_Wr, L0_attn_Wo, L0_attn_cmk, L0_attn_cmr, L0_attn_Wck, L0_attn_Wcv, L0_attn_Wcr, L0_xattn_Wq, L0_xattn_Wk, L0_xattn_Wv, L0_xattn_Wo, L0_ffn_router_W, L0_ffn_router_b, L0_ffn_gate_bias, L0_ffn_exp_Wup, L0_ffn_exp_bup, L0_ffn_exp_Wg, L0_ffn_exp_bg, L0_ffn_exp_Wdown, L0_ffn_exp_bdown, L0_ffn_share_Wup, L0_ffn_share_bup, L0_ffn_share_Wg, L0_ffn_share_bg, L0_ffn_share_Wdown, L0_ffn_share_bdown, L0_ffn_norm_w):
    import jax
    import jax.numpy as jnp

    def _L0_attn_ref(x, ln0_w, ln0_b, ln1_w, ln1_b, ln2_w, ln2_b, time_decay, time_first, tmk, tmv, tmr, Wk, Wv, Wr, Wo, cmk, cmr, Wck, Wcv, Wcr):
        import jax, jax.numpy as jnp
        import numpy as np
        from jax import lax
        L, B, T, C, F = (4, 4, 256, 128, 512)
        EPS = 1e-05

        def layernorm(x, w, b):
            m = jnp.mean(x, axis=-1, keepdims=True)
            v = jnp.var(x, axis=-1, keepdims=True)
            return (x - m) * lax.rsqrt(v + EPS) * w + b

        def time_shift(x):
            return jnp.pad(x, ((0, 0), (1, 0), (0, 0)))[:, :-1]

        def wkv(time_decay, time_first, k, v):
            w = -jnp.exp(time_decay)
            u = time_first
            kt = jnp.swapaxes(k, 0, 1)
            vt = jnp.swapaxes(v, 0, 1)
            Bn, Cn = (k.shape[0], k.shape[2])
            init = (jnp.zeros((Bn, Cn), k.dtype), jnp.zeros((Bn, Cn), k.dtype), jnp.full((Bn, Cn), -1e+38, k.dtype))

            def step(carry, kv):
                aa, bb, pp = carry
                kk, vv = kv
                ww = u + kk
                qq = jnp.maximum(pp, ww)
                e1 = jnp.exp(pp - qq)
                e2 = jnp.exp(ww - qq)
                out = (e1 * aa + e2 * vv) / (e1 * bb + e2)
                ww2 = pp + w
                qq2 = jnp.maximum(ww2, kk)
                e1b = jnp.exp(ww2 - qq2)
                e2b = jnp.exp(kk - qq2)
                return ((e1b * aa + e2b * vv, e1b * bb + e2b, qq2), out)
            _, out = lax.scan(step, init, (kt, vt))
            return jnp.swapaxes(out, 0, 1)
        x = layernorm(x, ln0_w, ln0_b)
        for l in range(L):
            h = layernorm(x, ln1_w[l], ln1_b[l])
            hh = time_shift(h)
            xk = h * tmk[l] + hh * (1 - tmk[l])
            xv = h * tmv[l] + hh * (1 - tmv[l])
            xr = h * tmr[l] + hh * (1 - tmr[l])
            k = jnp.einsum('btc,oc->bto', xk, Wk[l])
            v = jnp.einsum('btc,oc->bto', xv, Wv[l])
            sr = jax.nn.sigmoid(jnp.einsum('btc,oc->bto', xr, Wr[l]))
            rwkv = sr * wkv(time_decay[l], time_first[l], k, v)
            x = x + jnp.einsum('bto,co->btc', rwkv, Wo[l])
            h = layernorm(x, ln2_w[l], ln2_b[l])
            hh = time_shift(h)
            xk = h * cmk[l] + hh * (1 - cmk[l])
            xr = h * cmr[l] + hh * (1 - cmr[l])
            kf = jnp.einsum('btc,fc->btf', xk, Wck[l])
            kf = jnp.square(jax.nn.relu(kf))
            kv = jnp.einsum('btf,cf->btc', kf, Wcv[l])
            x = x + jax.nn.sigmoid(jnp.einsum('btc,oc->bto', xr, Wcr[l])) * kv
        return x

    def _L0_xattn_ref(query, key, value, attention_bias, Wq, Wk, Wv, Wo):
        import jax, jax.numpy as jnp
        import numpy as np
        EMBED = 128
        NHEAD = 16
        HEAD_DIM = EMBED // NHEAD
        B, SQ, _ = query.shape
        SKV = key.shape[1]

        def proj(x, W, S):
            return (x @ W.T).reshape(B, S, NHEAD, HEAD_DIM).transpose(0, 2, 1, 3)
        q = proj(query, Wq, SQ)
        k = proj(key, Wk, SKV)
        v = proj(value, Wv, SKV)
        scores = jnp.einsum('bhqd,bhkd->bhqk', q, k) / np.sqrt(HEAD_DIM)
        scores = scores + attention_bias[:, None, None, :]
        probs = jax.nn.softmax(scores, axis=-1)
        out = jnp.einsum('bhqk,bhkd->bhqd', probs, v)
        out = out.transpose(0, 2, 1, 3).reshape(B, SQ, EMBED)
        return out @ Wo.T

    def _L0_ffn_ref(x, router_W, router_b, gate_bias, exp_Wup, exp_bup, exp_Wg, exp_bg, exp_Wdown, exp_bdown, share_Wup, share_bup, share_Wg, share_bg, share_Wdown, share_bdown, norm_w):
        import jax, jax.numpy as jnp
        import numpy as np
        H, I, E, NS, C = (128, 128, 6, 2, 2)
        TOPK = 2
        TEMP = 1.0
        EPS = 1e-06
        B, S, Hd = x.shape
        xf = x.reshape(-1, Hd)
        for j in range(C):
            residual = xf
            gate = (xf @ router_W[j] + router_b[j]) / TEMP
            biased = gate + gate_bias[j]
            _, ids = jax.lax.top_k(biased, TOPK)
            sel = (ids[:, :, None] == jnp.arange(E)[None, None, :]).any(axis=1)
            weights = jax.nn.softmax(jnp.where(sel, gate, -jnp.inf), axis=-1)
            h = jnp.einsum('nh,ehi->eni', xf, exp_Wup) + exp_bup[:, None, :]
            h = jax.nn.silu(jnp.einsum('eni,eij->enj', h, exp_Wg) + exp_bg[:, None, :]) * h
            eo = jnp.einsum('eni,eih->enh', h, exp_Wdown) + exp_bdown[:, None, :]
            combined = jnp.einsum('ne,enh->nh', weights, eo)
            s = (xf @ share_Wup + share_bup).reshape(-1, NS, I)
            s = jax.nn.silu(s @ share_Wg + share_bg) * s
            share_out = (s @ share_Wdown + share_bdown).sum(axis=1)
            z = combined + share_out
            y = residual + z
            y = y * jax.lax.rsqrt(jnp.mean(y * y, axis=-1, keepdims=True) + EPS) * norm_w[j]
            xf = y
        return xf.reshape(B, S, Hd)
    x = _layernorm(x + _L0_attn_ref(x, L0_attn_ln0_w, L0_attn_ln0_b, L0_attn_ln1_w, L0_attn_ln1_b, L0_attn_ln2_w, L0_attn_ln2_b, L0_attn_time_decay, L0_attn_time_first, L0_attn_tmk, L0_attn_tmv, L0_attn_tmr, L0_attn_Wk, L0_attn_Wv, L0_attn_Wr, L0_attn_Wo, L0_attn_cmk, L0_attn_cmr, L0_attn_Wck, L0_attn_Wcv, L0_attn_Wcr), axis=-1)
    x = _layernorm(x + _L0_xattn_ref(x, ctx_1024, ctx_1024, fside_BxS2_0, L0_xattn_Wq, L0_xattn_Wk, L0_xattn_Wv, L0_xattn_Wo), axis=-1)
    x = _layernorm(x + _L0_ffn_ref(x, L0_ffn_router_W, L0_ffn_router_b, L0_ffn_gate_bias, L0_ffn_exp_Wup, L0_ffn_exp_bup, L0_ffn_exp_Wg, L0_ffn_exp_bg, L0_ffn_exp_Wdown, L0_ffn_exp_bdown, L0_ffn_share_Wup, L0_ffn_share_bup, L0_ffn_share_Wg, L0_ffn_share_bg, L0_ffn_share_Wdown, L0_ffn_share_bdown, L0_ffn_norm_w), axis=-1)
    return x

_drawn_inputs = setup_inputs


def setup_inputs(seed=0):
    import zlib

    import numpy as np

    out = dict(_drawn_inputs(seed))
    spreads = {'L0_attn_ln0_w': (1.0, 0.2),
     'L0_attn_ln0_b': (0.0, 0.1),
     'L0_attn_ln1_w': (1.0, 0.6),
     'L0_attn_ln1_b': (0.0, 0.8),
     'L0_attn_ln2_w': (1.0, 0.6),
     'L0_attn_ln2_b': (0.0, 0.8),
     'L0_ffn_exp_bup': (0.0, 0.8),
     'L0_ffn_exp_bg': (0.0, 0.8),
     'L0_ffn_exp_bdown': (0.0, 0.376),
     'L0_ffn_share_bup': (0.0, 0.8),
     'L0_ffn_share_bg': (0.0, 0.8),
     'L0_ffn_share_bdown': (0.0, 0.3),
     'L0_ffn_norm_w': (1.0, 0.2)}
    factors = {'L0_attn_time_decay': 8.0,
     'L0_attn_time_first': 8.0,
     'L0_attn_tmk': 8.0,
     'L0_attn_tmv': 8.0,
     'L0_attn_tmr': 8.0,
     'L0_attn_Wk': 8.0,
     'L0_attn_Wv': 4.1,
     'L0_attn_Wr': 8.0,
     'L0_attn_Wo': 4.07,
     'L0_attn_cmk': 8.0,
     'L0_attn_cmr': 8.0,
     'L0_attn_Wck': 6.133,
     'L0_attn_Wcv': 5.52,
     'L0_attn_Wcr': 8.0,
     'L0_ffn_router_b': 5.109,
     'L0_ffn_gate_bias': 4.279,
     'L0_ffn_exp_Wup': 8.0,
     'L0_ffn_exp_Wg': 8.0,
     'L0_ffn_exp_Wdown': 8.0,
     'L0_ffn_share_Wup': 8.0,
     'L0_ffn_share_Wg': 8.0,
     'L0_ffn_share_Wdown': 8.0}
    for name, (base, spread) in spreads.items():
        noise = np.random.default_rng([zlib.crc32(name.encode()), seed]).standard_normal(out[name].shape)
        drawn = base * np.exp(spread * noise) if base else spread * noise
        out[name] = jnp.asarray(drawn.astype(out[name].dtype))
    for name, factor in factors.items():
        out[name] = (out[name] * factor).astype(out[name].dtype)
    return out
```

```python
from contextlib import ExitStack

import concourse.bass as bass
from concourse import mybir

P = 128
LAYERS = 4
ROWS = 4
N = ROWS * P
PAD = P + 1
STREAMS = 2
HEADS = 16
HEAD = P // HEADS
GROUPS = HEADS // 4
EXPERTS = 6
SHARED = 2
ROUNDS = 2
FF = 4
EPS = 1e-5
RMS_EPS = 1e-6
FAR = -1e38
TOP = 40.0

F32 = mybir.dt.float32
F32R = mybir.dt.float32r
ALU = mybir.AluOpType
ACT = mybir.ActivationFunctionType
AX = mybir.AxisListType

VEC = {name: 4 * n for n, name in enumerate(
    ["ln1_w", "ln1_b", "ln2_w", "ln2_b", "decay", "first", "tmk", "tmv", "tmr", "cmk", "cmr"])}
VEC_BUP, VEC_SBUP, VEC_BG, VEC_SBG, VEC_N = 44, 50, 52, 58, 59
WR, WK, WV, WO, WCR, WCK, WCV, LAYER_W = 0, 1, 2, 3, 4, 5, 9, 13
UNITS = SHARED + EXPERTS
ROW_LN0W, ROW_LN0B, ROW_NORM, ROW_RB, ROW_GB = 0, P, 2 * P, 4 * P, 4 * P + ROUNDS * EXPERTS
ROW_N = ROW_GB + ROUNDS * EXPERTS
WROWS = 2 * EXPERTS + SHARED

SIGNALS = [
    "x_loaded", "ctx_loaded", "bias_loaded", "stored",
    "var", "rstd", "xn", "xT", "h", "mixed", "r_ready", "k_ready", "v_ready", "sr", "kp", "args",
    "decays", "den", "inv", "act_own", "rwkv", "wo", "mixed2", "kf", "relu", "squared", "cr", "sig", "cv", "x_new",
    "qT", "kT", "vT", "k_kept", "high", "low", "vext", "dup", "dup_out", "bias_split", "s_ready", "s_max",
    "mT", "mT_out", "st_ready", "probs", "pv", "heads_out", "oT", "oT_out", "attn",
    "gate", "gate_max", "gate_exp", "w_split", "wT", "wT_out", "up", "h_out", "g_ready", "silu", "wb", "t_out",
    "z_part", "z_done",
]


def network(nc, xs, ctxT, biasT, bias_rows, wl, wx, we, wrout, vec, rows, bdown, const, dup, out):
    PAIRS = xs.shape[0] // (ROWS * STREAMS)
    with ExitStack() as ctx:
        def sb(name, shape, dt=F32):
            return ctx.enter_context(nc.sbuf_tensor(name, shape, dt))

        def per_stream(name, shape, dt=F32):
            return [sb(f"{name}{s}", shape, dt) for s in range(STREAMS)]

        W = sb("W", [P, LAYERS * LAYER_W, P])
        WX = sb("WX", [P, 4, P])
        WE = sb("WE", [P, UNITS * 3, P])
        WROUT = sb("WROUT", [P, ROUNDS * EXPERTS])
        VECS = sb("VECS", [P, VEC_N])
        ROWB = sb("ROWB", [P, ROW_N])
        BDOWN = sb("BDOWN", [WROWS, P])
        CONST = sb("CONST", [P, P + 64])
        IDENT = CONST[:, 0:P]
        LOWER = CONST[:, P:P + EXPERTS * EXPERTS]
        PART = CONST[:, P + 36:P + 37]
        DUP = sb("DUP", [P, 4 * GROUPS, P], F32R)
        ONES2 = sb("ONES2", [P, P], F32R)
        NEGEYE = sb("NEGEYE", [P, GROUPS], F32R)
        WSEL = sb("WSEL", [WROWS, EXPERTS], F32R)
        NEGW = sb("NEGW", [P, LAYERS])
        ZTOP = sb("ZTOP", [P, LAYERS])
        WPAD = sb("WPAD", [P, LAYERS, ROWS * PAD])
        HALF = sb("HALF", [P, ROWS])

        x0 = per_stream("x0", [P, ROWS, P])
        x = per_stream("x", [P, ROWS, P])
        xn = per_stream("xn", [P, ROWS, P])
        hp = per_stream("hp", [P, ROWS, PAD])
        dh = per_stream("dh", [P, ROWS, P])
        mr = per_stream("mr", [P, N])
        mk = per_stream("mk", [P, N])
        mv = per_stream("mv", [P, N])
        sr = per_stream("sr", [P, N])
        kp = per_stream("kp", [P, ROWS, PAD])
        pp = per_stream("pp", [P, ROWS, PAD])
        aa = per_stream("aa", [P, ROWS, PAD])
        cc = per_stream("cc", [P, ROWS, PAD])
        cv = per_stream("cv", [P, ROWS, PAD])
        sa = per_stream("sa", [P, ROWS, PAD])
        sbb = per_stream("sbb", [P, ROWS, PAD])
        num = per_stream("num", [P, ROWS, P])
        kf = per_stream("kf", [P, FF, N])
        stats = per_stream("stats", [P, ROWS, 6])
        mvar = per_stream("mvar", [P, ROWS, 2])
        veps = per_stream("veps", [P, ROWS])
        rstd = per_stream("rstd", [P, ROWS])
        msq = per_stream("msq", [P, ROWS])

        ctxs = per_stream("ctxs", [P, N])
        hi = per_stream("hi", [P, N], F32R)
        lo = per_stream("lo", [P, N], F32R)
        qs = per_stream("qs", [P, GROUPS, N], F32R)
        ks = per_stream("ks", [P, GROUPS, N], F32R)
        vext = per_stream("vext", [P, ROWS, HEADS, HEAD + 1])
        kbias = per_stream("kbias", [P, ROWS])
        brow = per_stream("brow", [P, N])
        bsp = per_stream("bsp", [P, N], F32R)
        smax = per_stream("smax", [P, 4, 32])
        mT = per_stream("mT", [P, P], F32R)
        rsum = per_stream("rsum", [P, HEADS])

        gt = per_stream("gt", [P, ROWS, EXPERTS])
        bi = per_stream("bi", [P, ROWS, EXPERTS])
        cmp1 = per_stream("cmp1", [P, ROWS, EXPERTS * EXPERTS])
        cmp2 = per_stream("cmp2", [P, ROWS, EXPERTS * EXPERTS])
        rank = per_stream("rank", [P, ROWS, EXPERTS])
        gmax = per_stream("gmax", [P, ROWS])
        wts = per_stream("wts", [P, ROWS, WROWS])
        whi = per_stream("whi", [P, ROWS, EXPERTS], F32R)

        ps = [ctx.enter_context(nc.psum_tensor(f"ps{s}", [P, 4, N], F32)) for s in range(STREAMS)]

        def inner(t):
            return t[:, :, 1:PAD]

        def before(t):
            return t[:, :, 0:P]

        def flat(t):
            return t[:, :, :].rearrange("p b t -> p (b t)")

        ee = den = dh
        zz = [inner(t) for t in pp]
        bhi = lo
        wT = [t[0:WROWS, :] for t in hi]
        xa = xn
        xT = mr
        probs = kf
        heads = dh
        oT = mk
        h_e, silu_e, t_e = mk, mv, sr

        setup = {n: ctx.enter_context(nc.semaphore("set_" + n)) for n in
                 ("loads", "dup_loads", "pads", "consts", "own")}
        sig = {n: [ctx.enter_context(nc.semaphore(f"{n}{s}")) for s in range(STREAMS)] for n in SIGNALS}
        dve_own = [ctx.enter_context(nc.semaphore(f"dve_own{s}")) for s in range(STREAMS)]
        used = [q for pair in sig.values() for q in pair] + dve_own

        with nc.Block() as block:
            @block.sync
            def _(sp):
                sp.dma_start(VECS[:, :], vec).then_inc(setup["loads"], 16)
                sp.dma_start(CONST[:, :], const).then_inc(setup["loads"], 16)
                sp.dma_start(W[:, :, :], wl).then_inc(setup["loads"], 16)
                sp.dma_start(WX[:, :, :], wx).then_inc(setup["loads"], 16)
                sp.wait_ge(setup["loads"], 16 * 4)

            @block.scalar
            def _(act):
                for half in range(2):
                    act.dma_start(kf[half][:, 0:2, :].rearrange("p a b -> p (a b)"), dup[:, half, :]).then_inc(
                        setup["dup_loads"], 16)
                act.dma_start(WE[:, :, :], we).then_inc(setup["dup_loads"], 16)
                act.dma_start(WROUT[:, :], wrout).then_inc(setup["dup_loads"], 16)
                act.dma_start(ROWB[:, :], rows).then_inc(setup["dup_loads"], 16)
                act.dma_start(BDOWN[:, :], bdown).then_inc(setup["dup_loads"], 16)
                act.wait_ge(setup["loads"], 16 * 4)
                nc.scalar.activation(NEGW[:, :], VECS[:, VEC["decay"]:VEC["decay"] + LAYERS], ACT.Exp).then_inc(
                    setup["own"], 1)
                act.wait_ge(setup["dup_loads"], 16 * 6)

            @block.vector
            def _(dve):
                dve.wait_ge(setup["dup_loads"], 16 * 6)
                dve.wait_ge(setup["loads"], 16 * 4)
                for half in range(2):
                    nc.vector.tensor_copy(
                        DUP[:, 2 * GROUPS * half:2 * GROUPS * (half + 1), :].rearrange("p a b -> p (a b)"),
                        kf[half][:, 0:2, :].rearrange("p a b -> p (a b)"))
                nc.vector.tensor_copy(ONES2[:, :], CONST[:, P + 38:P + 39].broadcast_to([P, P]))
                nc.vector.tensor_copy(NEGEYE[:, :], CONST[:, P + 48:P + 48 + GROUPS])
                nc.vector.tensor_copy(WSEL[:, :], CONST[0:WROWS, P + 40:P + 40 + EXPERTS])
                nc.vector.memset(HALF[:, :], -0.5)
                nc.vector.tensor_scalar(ZTOP[:, :], VECS[:, VEC["first"]:VEC["first"] + LAYERS], -1.0, TOP,
                                        ALU.mult, ALU.add)
                for s in range(STREAMS):
                    nc.vector.memset(vext[s][:, :, :, HEAD:HEAD + 1], 1.0)
                    nc.vector.memset(wts[s][:, :, 2 * EXPERTS:WROWS], 1.0)
                dve.wait_ge(setup["own"], 1)
                dve.wait_ge(setup["pads"], 1)
                for l in range(LAYERS):
                    nc.vector.tensor_scalar(WPAD[:, l, :], WPAD[:, l, :], NEGW[:, l:l + 1], None,
                                            ALU.subtract).then_inc(setup["consts"], 1)
                dve.wait_ge(setup["consts"], LAYERS)
                wp = WPAD[:, :, :].rearrange("p l (b t) -> p (l b) t", t=PAD)
                nc.vector.memset(wp[:, :, 0:1], FAR)

            @block.gpsimd
            def _(pool):
                nc.gpsimd.memset(WPAD[:, :, :], 0.0).then_inc(setup["pads"], 1)
                for s in range(STREAMS):
                    nc.gpsimd.memset(hp[s][:, :, 0:1], 0.0)
                    nc.gpsimd.memset(kp[s][:, :, 0:1], FAR)
                    nc.gpsimd.memset(smax[s][:, :, :], 0.0)
                    for t in (aa, cc, cv):
                        nc.gpsimd.memset(t[s][:, :, 0:1], 0.0)

        with nc.Fori(0, PAIRS) as pair:
            with nc.Block() as block:
                both = range(STREAMS)

                @block.sync
                def _(sp):
                    for s in both:
                        first = pair * (STREAMS * ROWS) + s * ROWS
                        sp.dma_start(x0[s][:, :, :], xs[bass.ds(first, ROWS), :, :].rearrange("b t c -> t b c")
                                     ).then_inc(sig["x_loaded"][s], 16)
                    for s in both:
                        first = pair * (STREAMS * ROWS) + s * ROWS
                        sp.dma_start(ctxs[s][:, :], ctxT[:, bass.ds(first * P, N)]).then_inc(
                            sig["ctx_loaded"][s], 16)
                        sp.dma_start(brow[s][:, :], bias_rows[:, bass.ds(first * P, N)]).then_inc(
                            sig["bias_loaded"][s], 16)
                        sp.dma_start(kbias[s][:, :], biasT[:, bass.ds(first, ROWS)]).then_inc(
                            sig["bias_loaded"][s], 16)
                    for s in both:
                        first = pair * (STREAMS * ROWS) + s * ROWS
                        sp.wait_ge(sig["xn"][s], 2 * LAYERS + 4)
                        sp.dma_start(out[bass.ds(first, ROWS), :, :].rearrange("b t c -> t b c"), xn[s][:, :, :]
                                     ).then_inc(sig["stored"][s], 16)
                    for s in both:
                        sp.wait_ge(sig["stored"][s], 16)

                @block.gpsimd
                def _(pool):
                    norms = 1 + 2 * LAYERS + 2 + ROUNDS + 1
                    for n in range(norms):
                        for s in both:
                            pool.wait_ge(sig["var"][s], n + 1)
                            nc.gpsimd.tensor_tensor(rstd[s][:, :], veps[s][:, :], HALF[:, :], ALU.pow).then_inc(
                                sig["rstd"][s], 1)

                @block.tensor
                def _(pe):
                    def transposes(s, src, bank):
                        for b in range(ROWS):
                            last = nc.tensor.transpose(ps[s][:, bank, b * P:(b + 1) * P], src[s][:, b, :], IDENT)
                        return last

                    def token_major(s, src, w, bank, first=True, stop=True):
                        for b in range(ROWS):
                            last = nc.tensor.matmul(ps[s][:, bank, b * P:(b + 1) * P], src[:, b * P:(b + 1) * P], w,
                                                    start=first and b == 0, stop=stop, skip_group_check=True)
                        return last

                    def product(s, w, src, bank, start=True, stop=True):
                        return nc.tensor.matmul(ps[s][:, bank, :], w, src, start=start, stop=stop)

                    for l in range(LAYERS):
                        w = LAYER_W * l
                        for s in both:
                            pe.wait_ge(sig["xn"][s], 2 * l + 1)
                            transposes(s, xn, 0).then_inc(sig["xT"][s], 1)
                        for s in both:
                            pe.wait_ge(sig["mixed"][s], 3 * l + 1)
                            product(s, W[:, w + WK, :], mk[s][:, :], 1).then_inc(sig["k_ready"][s], 1)
                            pe.wait_ge(sig["mixed"][s], 3 * l + 2)
                            product(s, W[:, w + WV, :], mv[s][:, :], 2).then_inc(sig["v_ready"][s], 1)
                            pe.wait_ge(sig["mixed"][s], 3 * l + 3)
                            product(s, W[:, w + WR, :], mr[s][:, :], 3).then_inc(sig["r_ready"][s], 1)
                        for s in both:
                            pe.wait_ge(sig["rwkv"][s], l + 1)
                            token_major(s, num[s][:, :, :].rearrange("p b t -> p (b t)"), W[:, w + WO, :], 0).then_inc(
                                sig["wo"][s], 1)
                        for s in both:
                            pe.wait_ge(sig["xn"][s], 2 * l + 2)
                            transposes(s, xn, 0).then_inc(sig["xT"][s], 1)
                        for s in both:
                            pe.wait_ge(sig["mixed2"][s], 2 * l + 1)
                            for f in range(FF):
                                product(s, W[:, w + WCK + f, :], mk[s][:, :], f).then_inc(sig["kf"][s], 1)
                        for s in both:
                            pe.wait_ge(sig["mixed2"][s], 2 * l + 2)
                            pe.wait_ge(sig["relu"][s], FF * l + 1)
                            token_major(s, mr[s], W[:, w + WCR, :], 0).then_inc(sig["cr"][s], 1)
                            for f in range(FF):
                                pe.wait_ge(sig["squared"][s], FF * l + f + 1)
                                last = token_major(s, kf[s][:, f, :], W[:, w + WCV + f, :], 1, f == 0, f == FF - 1)
                            last.then_inc(sig["cv"][s], 1)

                    for s in both:
                        pe.wait_ge(sig["xn"][s], 2 * LAYERS + 1)
                        transposes(s, xn, 0).then_inc(sig["xT"][s], 1)
                    for s in both:
                        pe.wait_ge(sig["ctx_loaded"][s], 16)
                        product(s, WX[:, 1, :], ctxs[s][:, :], 2).then_inc(sig["kT"][s], 1)
                        token_major(s, ctxs[s], WX[:, 2, :], 3).then_inc(sig["vT"][s], 1)
                        pe.wait_ge(sig["h"][s], 2 * LAYERS + 1)
                        product(s, WX[:, 0, :], xT[s][:, :], 1).then_inc(sig["qT"][s], 1)
                    for which in range(2):
                        for s in both:
                            pe.wait_ge(sig["high"][s], which + 1)
                            pe.wait_ge(sig["low"][s], which + 1)
                            if which == 0:
                                pe.wait_ge(sig["vext"][s], 1)
                                pe.wait_ge(sig["k_kept"][s], 1)
                            for t in range(GROUPS):
                                if which == 1:
                                    pe.wait_ge(sig["dup_out"][s], t + 1)
                                at = 2 * GROUPS * which + t
                                nc.tensor.matmul(ps[s][:, t, :], DUP[:, at, :], hi[s][:, :], start=True, stop=False)
                                nc.tensor.matmul(ps[s][:, t, :], DUP[:, at + GROUPS, :], lo[s][:, :], start=False,
                                                 stop=True).then_inc(sig["dup"][s], 1)
                    for b in range(ROWS):
                        toks = slice(b * P, (b + 1) * P)
                        for s in both:
                            if b == 0:
                                pe.wait_ge(sig["dup_out"][s], 2 * GROUPS)
                                pe.wait_ge(sig["bias_split"][s], 1)
                            else:
                                pe.wait_ge(sig["heads_out"][s], b)
                            for g in range(4):
                                parts = slice(32 * g, 32 * g + 2)
                                bias = bsp[s][parts, toks].unsqueeze(1).broadcast_to([2, 4, P])
                                nc.tensor.matmul(ps[s][:, g, :].rearrange("p (t k) -> p t k", t=4), ONES2[parts, :], bias,
                                                 start=True, stop=False, skip_group_check=True)
                            for t in range(GROUPS):
                                for g in range(4):
                                    rows_ = slice(32 * g, 32 * g + 32)
                                    last = nc.tensor.matmul(ps[s][:, g, t * P:(t + 1) * P], qs[s][rows_, t, toks],
                                                            ks[s][rows_, t, toks], start=False, stop=t == GROUPS - 1,
                                                            skip_group_check=True)
                            last.then_inc(sig["s_ready"][s], 1)
                        for s in both:
                            pe.wait_ge(sig["s_max"][s], b + 1)
                            nc.tensor.transpose(ps[s][:, 0, 0:P], smax[s][:, :, :].rearrange("p g t -> p (g t)"), IDENT).then_inc(sig["mT"][s], 1)
                        for s in both:
                            pe.wait_ge(sig["mT_out"][s], b + 1)
                            for g in range(4):
                                for t in range(GROUPS):
                                    rows_ = slice(32 * g, 32 * g + GROUPS)
                                    nc.tensor.matmul(ps[s][:, g, t * P:(t + 1) * P],
                                                     NEGEYE[rows_, t:t + 1].broadcast_to([GROUPS, P]),
                                                     mT[s][rows_, :], start=t == 0, stop=False, skip_group_check=True)
                            for t in range(GROUPS):
                                for g in range(4):
                                    rows_ = slice(32 * g, 32 * g + 32)
                                    last = nc.tensor.matmul(ps[s][:, g, t * P:(t + 1) * P], ks[s][rows_, t, toks],
                                                            qs[s][rows_, t, toks], start=False, stop=t == GROUPS - 1,
                                                            skip_group_check=True)
                            last.then_inc(sig["st_ready"][s], 1)
                        for s in both:
                            pe.wait_ge(sig["probs"][s], b + 1)
                            for g in range(4):
                                for t in range(GROUPS):
                                    h = 4 * t + g
                                    last = nc.tensor.matmul(
                                        ps[s][:, 0, h * (HEAD + 1):(h + 1) * (HEAD + 1)],
                                        probs[s][:, g, t * P:(t + 1) * P], vext[s][:, b, h, :],
                                        start=g == 0 and t == 0, stop=True, skip_group_check=True)
                            last.then_inc(sig["pv"][s], 1)
                    for s in both:
                        pe.wait_ge(sig["heads_out"][s], ROWS)
                        transposes(s, heads, 0).then_inc(sig["oT"][s], 1)
                    for s in both:
                        pe.wait_ge(sig["oT_out"][s], 1)
                        token_major(s, oT[s], WX[:, 3, :], 1).then_inc(sig["attn"][s], 1)

                    for j in range(ROUNDS):
                        for s in both:
                            if j == 0:
                                pe.wait_ge(sig["xn"][s], 2 * LAYERS + 2)
                            else:
                                pe.wait_ge(sig["x_new"][s], j)
                            transposes(s, x if j else xn, 0).then_inc(sig["xT"][s], 1)
                        for s in both:
                            pe.wait_ge(sig["h"][s], 2 * LAYERS + 2 + j)
                            for b in range(ROWS):
                                last = nc.tensor.matmul(ps[s][:, 2, b * EXPERTS:(b + 1) * EXPERTS],
                                                        xT[s][:, b * P:(b + 1) * P],
                                                        WROUT[:, j * EXPERTS:(j + 1) * EXPERTS],
                                                        start=b == 0, stop=True, skip_group_check=True)
                            last.then_inc(sig["gate"][s], 1)
                        for u in range(UNITS):
                            n = UNITS * j + u
                            for s in both:
                                if u:
                                    pe.wait_ge(sig["silu"][s], n)
                                product(s, WE[:, u, :], xT[s][:, :], 0).then_inc(sig["up"][s], 1)
                            if u == SHARED:
                                for s in both:
                                    pe.wait_ge(sig["w_split"][s], j + 1)
                                    for b in range(ROWS):
                                        last = nc.tensor.transpose(ps[s][0:WROWS, 2, b * P:(b + 1) * P], wts[s][:, b, :],
                                                                   IDENT)
                                    last.then_inc(sig["wT"][s], 1)
                            for s in both:
                                pe.wait_ge(sig["h_out"][s], n + 1)
                                product(s, WE[:, UNITS + u, :], h_e[s][:, :], 1).then_inc(sig["g_ready"][s], 1)
                            for s in both:
                                if u >= SHARED:
                                    if u == SHARED:
                                        pe.wait_ge(sig["wT_out"][s], j + 1)
                                    else:
                                        pe.wait_ge(sig["t_out"][s], n)
                                    product(s, WSEL[:, u - SHARED:u - SHARED + 1].broadcast_to([WROWS, P]), wT[s][:, :],
                                            2).then_inc(sig["wb"][s], 1)
                            for s in both:
                                pe.wait_ge(sig["t_out"][s], n + 1)
                                token_major(s, t_e[s], WE[:, 2 * UNITS + u, :], 3, u == 0, False).then_inc(
                                    sig["z_part"][s], 1)
                        for s in both:
                            for b in range(ROWS):
                                last = nc.tensor.matmul(ps[s][:, 3, b * P:(b + 1) * P],
                                                        wT[s][:, b * P:(b + 1) * P].bitcast(F32), BDOWN[:, :],
                                                        start=False, stop=True, skip_group_check=True)
                            last.then_inc(sig["z_done"][s], 1)

                @block.scalar
                def _(act):
                    own = [0, 0]

                    for l in range(LAYERS):
                        def vecs(name):
                            return VECS[:, VEC[name] + l:VEC[name] + l + 1]

                        for half, (wn, bn) in enumerate((("ln1_w", "ln1_b"), ("ln2_w", "ln2_b"))):
                            for s in both:
                                pe_n = 2 * l + half + 1
                                act.wait_ge(sig["xT"][s], pe_n)
                                nc.scalar.activation(inner(hp[s]), ps[s][:, 0, :].rearrange("p (b t) -> p b t", t=P),
                                                     ACT.Identity, scale=vecs(wn), bias=vecs(bn)).then_inc(
                                    sig["h"][s], 1)
                            if half == 1:
                                break
                            for s in both:
                                act.wait_ge(sig["k_ready"][s], l + 1)
                                nc.scalar.activation(inner(kp[s]), ps[s][:, 1, :].rearrange("p (b t) -> p b t", t=P),
                                                     ACT.Identity).then_inc(sig["kp"][s], 1)
                            for s in both:
                                act.wait_ge(sig["r_ready"][s], l + 1)
                                nc.scalar.activation(sr[s][:, :], ps[s][:, 3, :], ACT.Sigmoid).then_inc(sig["sr"][s], 1)
                            for s in both:
                                act.wait_ge(sig["args"][s], 3 * l + 1)
                                nc.scalar.activation(inner(cc[s]), inner(cc[s]), ACT.Exp).then_inc(sig["decays"][s], 1)
                                act.wait_ge(sig["args"][s], 3 * l + 2)
                                nc.scalar.activation(inner(aa[s]), inner(aa[s]), ACT.Exp, scale=-1.0).then_inc(
                                    sig["decays"][s], 1)
                                act.wait_ge(sig["args"][s], 3 * l + 3)
                                nc.scalar.activation(zz[s][:, :, :], zz[s][:, :, :], ACT.Exp,
                                                     bias=vecs("first")).then_inc(sig["decays"][s], 1)
                            for s in both:
                                act.wait_ge(sig["den"][s], l + 1)
                                nc.scalar.activation(den[s][:, :, :], den[s][:, :, :], ACT.Ln).then_inc(
                                    sig["act_own"][s], 1)
                                own[s] += 1
                            for s in both:
                                act.wait_ge(sig["act_own"][s], own[s])
                                nc.scalar.activation(den[s][:, :, :], den[s][:, :, :], ACT.Exp, scale=-1.0).then_inc(
                                    sig["inv"][s], 1)
                        for s in both:
                            for f in range(FF):
                                act.wait_ge(sig["kf"][s], FF * l + f + 1)
                                nc.scalar.activation(kf[s][:, f, :], ps[s][:, f, :], ACT.Relu).then_inc(
                                    sig["relu"][s], 1)
                            for f in range(FF):
                                act.wait_ge(sig["relu"][s], FF * l + f + 1)
                                nc.scalar.activation(kf[s][:, f, :], kf[s][:, f, :], ACT.Square).then_inc(
                                    sig["squared"][s], 1)
                        for s in both:
                            act.wait_ge(sig["cr"][s], l + 1)
                            nc.scalar.activation(sr[s][:, :], ps[s][:, 0, :], ACT.Sigmoid).then_inc(sig["sig"][s], 1)

                    for s in both:
                        act.wait_ge(sig["xT"][s], 2 * LAYERS + 1)
                        nc.scalar.activation(xT[s][:, :], ps[s][:, 0, :], ACT.Identity).then_inc(sig["h"][s], 1)
                    for s in both:
                        act.wait_ge(sig["vT"][s], 1)
                        nc.scalar.activation(vext[s][:, :, :, 0:HEAD],
                                             ps[s][:, 3, :].rearrange("p (b h d) -> p b h d", b=ROWS, d=HEAD),
                                             ACT.Identity).then_inc(sig["vext"][s], 1)
                    for which in range(2):
                        for s in both:
                            if which == 0:
                                act.wait_ge(sig["qT"][s], 1)
                            else:
                                act.wait_ge(sig["low"][s], 1)
                                act.wait_ge(sig["k_kept"][s], 1)
                                act.wait_ge(sig["dup"][s], GROUPS)
                            source = ps[s][:, 1, :] if which == 0 else mv[s][:, :]
                            nc.scalar.activation(hi[s][:, :], source, ACT.Identity).then_inc(sig["high"][s], 1)
                            if which == 0:
                                act.wait_ge(sig["kT"][s], 1)
                                nc.scalar.activation(mv[s][:, :], ps[s][:, 2, :], ACT.Identity).then_inc(
                                    sig["k_kept"][s], 1)
                        for s in both:
                            dst = ks if which else qs
                            for t in range(GROUPS):
                                act.wait_ge(sig["dup"][s], GROUPS * which + t + 1)
                                nc.scalar.activation(dst[s][:, t, :], ps[s][:, t, :], ACT.Identity).then_inc(
                                    sig["dup_out"][s], 1)
                    for b in range(ROWS):
                        for s in both:
                            act.wait_ge(sig["mT"][s], b + 1)
                            nc.scalar.activation(mT[s][:, :], ps[s][:, 0, 0:P], ACT.Identity).then_inc(
                                sig["mT_out"][s], 1)
                        for s in both:
                            act.wait_ge(sig["st_ready"][s], b + 1)
                            act.wait_ge(sig["bias_loaded"][s], 32)
                            if b:
                                act.wait_ge(sig["pv"][s], b)
                            nc.scalar.activation(probs[s][:, :, :].rearrange("p a b -> p (a b)"),
                                                 ps[s][:, :, :].rearrange("p a b -> p (a b)"), ACT.Exp,
                                                 bias=kbias[s][:, b:b + 1], scale=HEAD ** -0.5).then_inc(
                                sig["probs"][s], 1)
                    for s in both:
                        act.wait_ge(sig["oT"][s], 1)
                        nc.scalar.activation(oT[s][:, :], ps[s][:, 0, :], ACT.Identity).then_inc(sig["oT_out"][s], 1)

                    for j in range(ROUNDS):
                        for s in both:
                            act.wait_ge(sig["xT"][s], 2 * LAYERS + 2 + j)
                            nc.scalar.activation(xT[s][:, :], ps[s][:, 0, :], ACT.Identity).then_inc(sig["h"][s], 1)
                        for u in range(UNITS):
                            n = UNITS * j + u
                            col = u if u < SHARED else u - SHARED
                            up_b = (VEC_SBUP if u < SHARED else VEC_BUP) + col
                            g_b = VEC_SBG if u < SHARED else VEC_BG + col
                            for s in both:
                                act.wait_ge(sig["up"][s], n + 1)
                                if n:
                                    act.wait_ge(sig["t_out"][s], n)
                                nc.scalar.activation(h_e[s][:, :], ps[s][:, 0, :], ACT.Identity,
                                                     bias=VECS[:, up_b:up_b + 1]).then_inc(sig["h_out"][s], 1)
                            if u == 0:
                                for s in both:
                                    act.wait_ge(sig["gate_max"][s], j + 1)
                                    nc.scalar.activation(gt[s][:, :, :], gt[s][:, :, :], ACT.Exp).then_inc(
                                        sig["gate_exp"][s], 1)
                            if u == SHARED:
                                for s in both:
                                    act.wait_ge(sig["wT"][s], j + 1)
                                    nc.scalar.activation(wT[s][:, :], ps[s][0:WROWS, 2, :], ACT.Identity).then_inc(
                                        sig["wT_out"][s], 1)
                            for s in both:
                                act.wait_ge(sig["g_ready"][s], n + 1)
                                nc.scalar.activation(silu_e[s][:, :], ps[s][:, 1, :], ACT.Silu,
                                                     bias=VECS[:, g_b:g_b + 1]).then_inc(sig["silu"][s], 1)

                @block.vector
                def _(dve):
                    steps = [0, 0]
                    norms = [0, 0]

                    def done(s, ins):
                        ins.then_inc(dve_own[s], 1)
                        steps[s] += 1
                        return steps[s]

                    def need(s, n):
                        dve.wait_ge(dve_own[s], n)

                    def variances(s, src, eps, rms=False):
                        for b in range(ROWS):
                            n = done(s, nc.vector.bn_stats(stats[s][:, b, :], src[s][:, b, :]))
                        need(s, n)
                        for b in range(ROWS):
                            n = done(s, nc.vector.bn_aggr(mvar[s][:, b, :], stats[s][:, b, :]))
                        need(s, n)
                        if rms:
                            n = done(s, nc.vector.tensor_tensor(msq[s][:, :], mvar[s][:, :, 0], mvar[s][:, :, 0],
                                                                ALU.mult))
                            need(s, n)
                            nc.vector.scalar_tensor_tensor(veps[s][:, :], msq[s][:, :], eps, mvar[s][:, :, 1],
                                                           ALU.add, ALU.add).then_inc(sig["var"][s], 1)
                        else:
                            nc.vector.tensor_scalar(veps[s][:, :], mvar[s][:, :, 1], eps, None, ALU.add).then_inc(
                                sig["var"][s], 1)

                    def normed(s, dst, src):
                        norms[s] += 1
                        dve.wait_ge(sig["rstd"][s], norms[s])
                        for b in range(ROWS):
                            last = nc.vector.tensor_scalar(dst[s][:, b, :], src[s][:, b, :], mvar[s][:, b, 0:1],
                                                           rstd[s][:, b:b + 1], ALU.subtract, ALU.mult)
                        return last

                    for s in both:
                        dve.wait_ge(sig["x_loaded"][s], 16)
                        variances(s, x0, EPS)
                    for s in both:
                        need(s, done(s, normed(s, x, x0)))
                        row = ROWB[:, ROW_LN0W:ROW_LN0W + P].unsqueeze(1).broadcast_to([P, ROWS, P])
                        need(s, done(s, nc.vector.tensor_tensor(x[s][:, :, :], x[s][:, :, :], row, ALU.mult)))
                        row = ROWB[:, ROW_LN0B:ROW_LN0B + P].unsqueeze(1).broadcast_to([P, ROWS, P])
                        need(s, done(s, nc.vector.tensor_tensor(x[s][:, :, :], x[s][:, :, :], row, ALU.add)))
                        variances(s, x, EPS)

                    for l in range(LAYERS):
                        def vecs(name):
                            return VECS[:, VEC[name] + l:VEC[name] + l + 1]

                        def mix(s, dst, name):
                            return nc.vector.scalar_tensor_tensor(
                                dst[s][:, :].rearrange("p (b t) -> p b t", t=P), dh[s][:, :, :], vecs(name),
                                before(hp[s]), ALU.mult, ALU.add)

                        for s in both:
                            normed(s, xn, x).then_inc(sig["xn"][s], 1)
                        for s in both:
                            dve.wait_ge(sig["h"][s], 2 * l + 1)
                            need(s, done(s, nc.vector.tensor_tensor(dh[s][:, :, :], inner(hp[s]), before(hp[s]),
                                                                    ALU.subtract)))
                            mix(s, mk, "tmk").then_inc(sig["mixed"][s], 1)
                            mix(s, mv, "tmv").then_inc(sig["mixed"][s], 1)
                            mix(s, mr, "tmr").then_inc(sig["mixed"][s], 1)
                        for s in both:
                            dve.wait_ge(sig["kp"][s], l + 1)
                            need(s, done(s, nc.vector.tensor_tensor_scan(flat(pp[s]), WPAD[:, l, :], flat(kp[s]), FAR,
                                                                         ALU.add, ALU.max)))
                            need(s, done(s, nc.vector.tensor_tensor(ee[s][:, :, :], inner(kp[s]), before(pp[s]),
                                                                    ALU.subtract)))
                            nc.vector.tensor_scalar(inner(cc[s]), ee[s][:, :, :], NEGW[:, l:l + 1], 0.0, ALU.add,
                                                    ALU.min).then_inc(sig["args"][s], 1)
                            nc.vector.tensor_scalar(inner(aa[s]), ee[s][:, :, :], NEGW[:, l:l + 1], 0.0, ALU.add,
                                                    ALU.max).then_inc(sig["args"][s], 1)
                            nc.vector.tensor_scalar(zz[s][:, :, :], ee[s][:, :, :], ZTOP[:, l:l + 1], None,
                                                    ALU.min).then_inc(sig["args"][s], 1)
                        for s in both:
                            v = ps[s][:, 2, :].rearrange("p (b t) -> p b t", t=P)
                            dve.wait_ge(sig["v_ready"][s], l + 1)
                            dve.wait_ge(sig["decays"][s], 3 * l + 2)
                            n_cv = done(s, nc.vector.tensor_tensor(inner(cv[s]), inner(cc[s]), v, ALU.mult))
                            n_b = done(s, nc.vector.tensor_tensor_scan(flat(sbb[s]), flat(aa[s]), flat(cc[s]), 0.0,
                                                                       ALU.mult, ALU.add))
                            dve.wait_ge(sig["decays"][s], 3 * l + 3)
                            n_zv = done(s, nc.vector.tensor_tensor(num[s][:, :, :], zz[s][:, :, :], v, ALU.mult))
                            need(s, n_b)
                            nc.vector.tensor_tensor(den[s][:, :, :], zz[s][:, :, :], before(sbb[s]), ALU.add).then_inc(
                                sig["den"][s], 1)
                            need(s, n_cv)
                            need(s, done(s, nc.vector.tensor_tensor_scan(flat(sa[s]), flat(aa[s]), flat(cv[s]), 0.0,
                                                                         ALU.mult, ALU.add)))
                            need(s, done(s, nc.vector.tensor_tensor(num[s][:, :, :], num[s][:, :, :], before(sa[s]),
                                                                    ALU.add)))
                            dve.wait_ge(sig["sr"][s], l + 1)
                            n_sr = done(s, nc.vector.tensor_tensor(
                                num[s][:, :, :], num[s][:, :, :], sr[s][:, :].rearrange("p (b t) -> p b t", t=P),
                                ALU.mult))
                        for s in both:
                            dve.wait_ge(sig["inv"][s], l + 1)
                            need(s, steps[s])
                            nc.vector.tensor_tensor(num[s][:, :, :], num[s][:, :, :], den[s][:, :, :],
                                                    ALU.mult).then_inc(sig["rwkv"][s], 1)
                        for s in both:
                            dve.wait_ge(sig["wo"][s], l + 1)
                            need(s, done(s, nc.vector.tensor_tensor(
                                x[s][:, :, :], x[s][:, :, :], ps[s][:, 0, :].rearrange("p (b t) -> p b t", t=P),
                                ALU.add)))
                            variances(s, x, EPS)
                        for s in both:
                            normed(s, xn, x).then_inc(sig["xn"][s], 1)
                        for s in both:
                            dve.wait_ge(sig["h"][s], 2 * l + 2)
                            need(s, done(s, nc.vector.tensor_tensor(dh[s][:, :, :], inner(hp[s]), before(hp[s]),
                                                                    ALU.subtract)))
                            mix(s, mk, "cmk").then_inc(sig["mixed2"][s], 1)
                            mix(s, mr, "cmr").then_inc(sig["mixed2"][s], 1)
                        for s in both:
                            dve.wait_ge(sig["sig"][s], l + 1)
                            dve.wait_ge(sig["cv"][s], l + 1)
                            need(s, done(s, nc.vector.tensor_tensor(sr[s][:, :], sr[s][:, :], ps[s][:, 1, :],
                                                                    ALU.mult)))
                            n = done(s, nc.vector.tensor_tensor(
                                x[s][:, :, :], x[s][:, :, :], sr[s][:, :].rearrange("p (b t) -> p b t", t=P), ALU.add))
                            need(s, n)
                            if l == LAYERS - 1:
                                need(s, done(s, nc.vector.tensor_tensor(x[s][:, :, :], x[s][:, :, :], x0[s][:, :, :],
                                                                        ALU.add)))
                            variances(s, x, EPS)

                    for s in both:
                        normed(s, xa, x).then_inc(sig["xn"][s], 1)
                    for s in both:
                        dve.wait_ge(sig["bias_loaded"][s], 32)
                        need(s, done(s, nc.vector.tensor_scalar(brow[s][:, :], brow[s][:, :], HEAD ** 0.5, None,
                                                                ALU.mult)))
                        need(s, done(s, nc.vector.tensor_copy(bhi[s][:, :], brow[s][:, :])))
                        need(s, done(s, nc.vector.tensor_scalar(bhi[s][:, :], bhi[s][:, :].bitcast(F32), PART, None,
                                                                ALU.mult)))
                        nc.vector.tensor_tensor(bsp[s][:, :], brow[s][:, :], bhi[s][:, :].bitcast(F32),
                                                ALU.subtract).then_inc(sig["bias_split"][s], 1)
                    for which in range(2):
                        for s in both:
                            dve.wait_ge(sig["high"][s], which + 1)
                            if which == 1:
                                dve.wait_ge(sig["dup"][s], GROUPS)
                            else:
                                dve.wait_ge(sig["bias_split"][s], 1)
                            source = ps[s][:, 1, :] if which == 0 else mv[s][:, :]
                            nc.vector.tensor_tensor(lo[s][:, :], source, hi[s][:, :].bitcast(F32),
                                                    ALU.subtract).then_inc(sig["low"][s], 1)
                    for b in range(ROWS):
                        for s in both:
                            dve.wait_ge(sig["s_ready"][s], b + 1)
                            nc.vector.tensor_reduce(smax[s][:, :, 0:GROUPS],
                                                    ps[s][:, :, :].rearrange("p g (t k) -> p g t k", k=P),
                                                    AX.X, ALU.max).then_inc(sig["s_max"][s], 1)
                        for s in both:
                            dve.wait_ge(sig["pv"][s], b + 1)
                            o = ps[s][:, 0, 0:HEADS * (HEAD + 1)].rearrange("p (h d) -> p h d", d=HEAD + 1)
                            need(s, done(s, nc.vector.reciprocal(rsum[s][:, :], o[:, :, HEAD])))
                            nc.vector.tensor_tensor(heads[s][:, b, :].rearrange("p (h d) -> p h d", d=HEAD),
                                                    o[:, :, 0:HEAD],
                                                    rsum[s][:, :].unsqueeze(2).broadcast_to([P, HEADS, HEAD]),
                                                    ALU.mult).then_inc(sig["heads_out"][s], 1)
                    for s in both:
                        dve.wait_ge(sig["attn"][s], 1)
                        need(s, done(s, nc.vector.tensor_tensor(
                            x[s][:, :, :], xa[s][:, :, :], ps[s][:, 1, :].rearrange("p (b t) -> p b t", t=P), ALU.add)))
                        variances(s, x, EPS)
                    for s in both:
                        normed(s, xa, x).then_inc(sig["xn"][s], 1)

                    for j in range(ROUNDS):
                        rb = ROWB[:, ROW_RB + j * EXPERTS:ROW_RB + (j + 1) * EXPERTS].unsqueeze(1).broadcast_to(
                            [P, ROWS, EXPERTS])
                        gb = ROWB[:, ROW_GB + j * EXPERTS:ROW_GB + (j + 1) * EXPERTS].unsqueeze(1).broadcast_to(
                            [P, ROWS, EXPERTS])
                        for s in both:
                            dve.wait_ge(sig["gate"][s], j + 1)
                            need(s, done(s, nc.vector.tensor_tensor(
                                gt[s][:, :, :], ps[s][:, 2, 0:ROWS * EXPERTS].rearrange("p (b e) -> p b e", e=EXPERTS),
                                rb, ALU.add)))
                            need(s, done(s, nc.vector.tensor_tensor(bi[s][:, :, :], gt[s][:, :, :], gb, ALU.add)))
                            for b in range(ROWS):
                                shape = [P, EXPERTS, EXPERTS]
                                other = bi[s][:, b, :].unsqueeze(1).broadcast_to(shape)
                                own = bi[s][:, b, :].unsqueeze(2).broadcast_to(shape)
                                c1 = cmp1[s][:, b, :].rearrange("p (e f) -> p e f", f=EXPERTS)
                                c2 = cmp2[s][:, b, :].rearrange("p (e f) -> p e f", f=EXPERTS)
                                done(s, nc.vector.tensor_tensor(c1, other, own, ALU.is_gt))
                                n = done(s, nc.vector.tensor_tensor(c2, other, own, ALU.is_equal))
                            need(s, n)
                            lower = LOWER.unsqueeze(1).broadcast_to([P, ROWS, EXPERTS * EXPERTS])
                            need(s, done(s, nc.vector.tensor_tensor(cmp2[s][:, :, :], cmp2[s][:, :, :], lower,
                                                                    ALU.mult)))
                            need(s, done(s, nc.vector.tensor_tensor(cmp1[s][:, :, :], cmp1[s][:, :, :],
                                                                    cmp2[s][:, :, :], ALU.add)))
                            need(s, done(s, nc.vector.tensor_reduce(
                                rank[s][:, :, :].rearrange("p b e -> p (b e)"),
                                cmp1[s][:, :, :].rearrange("p b (e f) -> p (b e) f", f=EXPERTS), AX.X, ALU.add)))
                            need(s, done(s, nc.vector.tensor_scalar(rank[s][:, :, :], rank[s][:, :, :], 1.5, -1e30,
                                                                    ALU.is_gt, ALU.mult)))
                            need(s, done(s, nc.vector.tensor_tensor(gt[s][:, :, :], gt[s][:, :, :], rank[s][:, :, :],
                                                                    ALU.add)))
                            need(s, done(s, nc.vector.tensor_reduce(gmax[s][:, :], gt[s][:, :, :], AX.X, ALU.max)))
                            nc.vector.tensor_tensor(gt[s][:, :, :], gt[s][:, :, :],
                                                    gmax[s][:, :].unsqueeze(2).broadcast_to([P, ROWS, EXPERTS]),
                                                    ALU.subtract).then_inc(sig["gate_max"][s], 1)
                        for s in both:
                            dve.wait_ge(sig["gate_exp"][s], j + 1)
                            need(s, done(s, nc.vector.tensor_reduce(gmax[s][:, :], gt[s][:, :, :], AX.X, ALU.add)))
                            need(s, done(s, nc.vector.reciprocal(gmax[s][:, :], gmax[s][:, :])))
                            need(s, done(s, nc.vector.tensor_tensor(
                                gt[s][:, :, :], gt[s][:, :, :],
                                gmax[s][:, :].unsqueeze(2).broadcast_to([P, ROWS, EXPERTS]), ALU.mult)))
                            need(s, done(s, nc.vector.tensor_copy(whi[s][:, :, :], gt[s][:, :, :])))
                            n1 = done(s, nc.vector.tensor_copy(wts[s][:, :, 0:EXPERTS], whi[s][:, :, :].bitcast(F32)))
                            need(s, n1)
                            nc.vector.tensor_tensor(wts[s][:, :, EXPERTS:2 * EXPERTS], gt[s][:, :, :],
                                                    whi[s][:, :, :].bitcast(F32), ALU.subtract).then_inc(
                                sig["w_split"][s], 1)
                        for u in range(UNITS):
                            n = UNITS * j + u
                            for s in both:
                                dve.wait_ge(sig["silu"][s], n + 1)
                                if n:
                                    dve.wait_ge(sig["z_part"][s], n)
                                mul = nc.vector.tensor_tensor(t_e[s][:, :], silu_e[s][:, :], h_e[s][:, :], ALU.mult)
                                if u < SHARED:
                                    mul.then_inc(sig["t_out"][s], 1)
                                else:
                                    need(s, done(s, mul))
                                    dve.wait_ge(sig["wb"][s], EXPERTS * j + u - SHARED + 1)
                                    nc.vector.tensor_tensor(t_e[s][:, :], t_e[s][:, :], ps[s][:, 2, :],
                                                            ALU.mult).then_inc(sig["t_out"][s], 1)
                        for s in both:
                            src = x if j else xa
                            dve.wait_ge(sig["z_done"][s], j + 1)
                            need(s, done(s, nc.vector.tensor_tensor(
                                x[s][:, :, :], src[s][:, :, :], ps[s][:, 3, :].rearrange("p (b t) -> p b t", t=P),
                                ALU.add)))
                            variances(s, x, RMS_EPS, rms=True)
                        for s in both:
                            norms[s] += 1
                            dve.wait_ge(sig["rstd"][s], norms[s])
                            for b in range(ROWS):
                                last = nc.vector.scalar_tensor_tensor(
                                    x[s][:, b, :], x[s][:, b, :], rstd[s][:, b:b + 1],
                                    ROWB[:, ROW_NORM + j * P:ROW_NORM + (j + 1) * P], ALU.mult, ALU.mult)
                            last.then_inc(sig["x_new"][s], 1)
                    for s in both:
                        dve.wait_ge(sig["x_new"][s], ROUNDS)
                        need(s, done(s, nc.vector.tensor_tensor(x[s][:, :, :], x[s][:, :, :], xa[s][:, :, :],
                                                                ALU.add)))
                        variances(s, x, EPS)
                    for s in both:
                        normed(s, xn, x).then_inc(sig["xn"][s], 2)
            nc.all_engine_barrier(sems_to_clear=range(used[0].num, used[-1].num + 1))


def kernel(**inputs):
    import numpy as np
    import concourse.bacc as bacc
    from concourse import mybir as mb
    from concourse.bass_utils import run_bass_kernel_spmd

    a = {k: np.asarray(v) for k, v in inputs.items()}
    r = {k[8:]: v for k, v in a.items() if k.startswith("L0_attn_")}
    t = {k[9:]: v for k, v in a.items() if k.startswith("L0_xattn_")}
    f = {k[7:]: v for k, v in a.items() if k.startswith("L0_ffn_")}

    def chunks(w):
        return [w[:, i:i + P] for i in range(0, w.shape[1], P)]

    wl = []
    for l in range(LAYERS):
        wl += [r[n][l].T for n in ("Wr", "Wk", "Wv", "Wo")] + [r["Wcr"][l].T] + chunks(r["Wck"][l].T)
        wl += [r["Wcv"][l].T[i:i + P] for i in range(0, FF * P, P)]
    wx = [t[n].T for n in ("Wq", "Wk", "Wv", "Wo")]
    we = chunks(f["share_Wup"]) + list(f["exp_Wup"]) + [f["share_Wg"]] * SHARED + list(f["exp_Wg"])
    we += [f["share_Wdown"]] * SHARED + list(f["exp_Wdown"])
    vec = [r[n].T for n in ("ln1_w", "ln1_b", "ln2_w", "ln2_b", "time_decay", "time_first", "tmk", "tmv", "tmr",
                            "cmk", "cmr")]
    vec += [f["exp_bup"].T, f["share_bup"].reshape(SHARED, P).T, f["exp_bg"].T, f["share_bg"].reshape(1, P).T]
    rows = np.concatenate([r["ln0_w"], r["ln0_b"], f["norm_w"].ravel(), f["router_b"].ravel(), f["gate_bias"].ravel()])
    bdown = np.concatenate([f["exp_bdown"], f["exp_bdown"], np.stack([f["share_bdown"]] * SHARED)])

    const = np.zeros((P, P + 64), np.float32)
    const[:, :P] = np.eye(P)
    const[:, P:P + 36] = np.tri(EXPERTS, k=-1).reshape(1, 36)
    const[1::2, P + 36] = 1.0
    const[:, P + 38] = 1.0
    for g in range(4):
        const[range(32 * g, 32 * g + GROUPS), range(P + 48, P + 48 + GROUPS)] = -1.0
    for e in range(EXPERTS):
        const[[e, EXPERTS + e], P + 40 + e] = 1.0
    dup = np.zeros((P, 2, 2, GROUPS, P), np.float32)
    for which, highs in enumerate(((0, 2), (0, 1))):
        for g in range(GROUPS):
            for place in range(4):
                for part in range(4):
                    for d in range(HEAD):
                        dup[HEAD * (4 * g + place) + d, which, int(part not in highs), g, 32 * place + 8 * part + d] = 1

    arrays = {
        "xs": a["x"],
        "ctxT": a["ctx_1024"].reshape(-1, P).T,
        "biasT": a["fside_BxS2_0"].T,
        "bias_rows": np.broadcast_to(a["fside_BxS2_0"].reshape(1, -1), (P, a["fside_BxS2_0"].size)),
        "wl": np.stack(wl, 1), "wx": np.stack(wx, 1), "we": np.stack(we, 1),
        "wrout": np.concatenate(list(f["router_W"]), 1),
        "vec": np.concatenate(vec, 1), "rows": np.broadcast_to(rows, (P, ROW_N)), "bdown": bdown,
        "const": const, "dup": dup.reshape(P, 2, 2 * GROUPS * P),
    }
    nc = bacc.Bacc("TRN2", target_bir_lowering=False, num_devices=1)
    arrays = {n: np.ascontiguousarray(v) for n, v in arrays.items()}
    args = [nc.dram_tensor(n, v.shape, mb.dt.from_np(v.dtype), kind="ExternalInput").ap() for n, v in arrays.items()]
    out = nc.dram_tensor("out", a["x"].shape, F32, kind="ExternalOutput").ap()
    network(nc, *args, out)
    result = run_bass_kernel_spmd(nc, [arrays], core_ids=[0])
    return result.results[0]["out"]
```

```python
from contextlib import ExitStack

import concourse.bass as bass
from concourse import mybir

P = 128
LAYERS = 4
ROWS = 4
N = ROWS * P
PAD = P + 1
STREAMS = 2
HEADS = 16
HEAD = P // HEADS
GROUPS = HEADS // 4
EXPERTS = 6
SHARED = 2
ROUNDS = 2
FF = 4
EPS = 1e-5
RMS_EPS = 1e-6
FAR = -1e38
TOP = 40.0

F32 = mybir.dt.float32
F32R = mybir.dt.float32r
ALU = mybir.AluOpType
ACT = mybir.ActivationFunctionType
AX = mybir.AxisListType

VEC = {name: 4 * n for n, name in enumerate(
    ["ln1_w", "ln1_b", "ln2_w", "ln2_b", "decay", "first", "tmk", "tmv", "tmr", "cmk", "cmr"])}
VEC_BUP, VEC_SBUP, VEC_BG, VEC_SBG, VEC_N = 44, 50, 52, 58, 59
WR, WK, WV, WO, WCR, WCK, WCV, LAYER_W = 0, 1, 2, 3, 4, 5, 9, 13
UNITS = SHARED + EXPERTS
ROW_LN0W, ROW_LN0B, ROW_NORM, ROW_RB, ROW_GB = 0, P, 2 * P, 4 * P, 4 * P + ROUNDS * EXPERTS
ROW_N = ROW_GB + ROUNDS * EXPERTS
WROWS = 2 * EXPERTS + SHARED

SIGNALS = [
    "x_loaded", "ctx_loaded", "bias_loaded", "stored",
    "var", "rstd", "xn", "xT", "h", "mixed", "r_ready", "k_ready", "v_ready", "sr", "kp", "args",
    "decays", "den", "inv", "act_own", "rwkv", "wo", "mixed2", "kf", "relu", "squared", "cr", "sig", "cv", "x_new",
    "qT", "kT", "vT", "k_kept", "high", "low", "vext", "dup", "dup_out", "bias_split", "s_ready", "s_max",
    "mT", "mT_out", "st_ready", "probs", "pv", "heads_out", "oT", "oT_out", "attn",
    "gate", "gate_max", "gate_exp", "w_split", "wT", "wT_out", "up", "h_out", "g_ready", "silu", "wb", "t_out",
    "z_part", "z_done",
]


def network(nc, xs, ctxT, biasT, bias_rows, wl, wx, we, wrout, vec, rows, bdown, const, dup, out):
    PAIRS = xs.shape[0] // (ROWS * STREAMS)
    with ExitStack() as ctx:
        def sb(name, shape, dt=F32):
            return ctx.enter_context(nc.sbuf_tensor(name, shape, dt))

        def per_stream(name, shape, dt=F32):
            return [sb(f"{name}{s}", shape, dt) for s in range(STREAMS)]

        W = sb("W", [P, LAYERS * LAYER_W, P])
        WX = sb("WX", [P, 4, P])
        WE = sb("WE", [P, UNITS * 3, P])
        WROUT = sb("WROUT", [P, ROUNDS * EXPERTS])
        VECS = sb("VECS", [P, VEC_N])
        ROWB = sb("ROWB", [P, ROW_N])
        BDOWN = sb("BDOWN", [WROWS, P])
        CONST = sb("CONST", [P, P + 64])
        IDENT = CONST[:, 0:P]
        LOWER = CONST[:, P:P + EXPERTS * EXPERTS]
        PART = CONST[:, P + 36:P + 37]
        DUP = sb("DUP", [P, 4 * GROUPS, P], F32R)
        ONES2 = sb("ONES2", [P, P], F32R)
        NEGEYE = sb("NEGEYE", [P, GROUPS], F32R)
        WSEL = sb("WSEL", [WROWS, EXPERTS], F32R)
        NEGW = sb("NEGW", [P, LAYERS])
        ZTOP = sb("ZTOP", [P, LAYERS])
        WPAD = sb("WPAD", [P, LAYERS, ROWS * PAD])
        HALF = sb("HALF", [P, ROWS])

        x0 = per_stream("x0", [P, ROWS, P])
        x = per_stream("x", [P, ROWS, P])
        xn = per_stream("xn", [P, ROWS, P])
        hp = per_stream("hp", [P, ROWS, PAD])
        dh = per_stream("dh", [P, ROWS, P])
        mr = per_stream("mr", [P, N])
        mk = per_stream("mk", [P, N])
        mv = per_stream("mv", [P, N])
        sr = per_stream("sr", [P, N])
        kp = per_stream("kp", [P, ROWS, PAD])
        pp = per_stream("pp", [P, ROWS, PAD])
        aa = per_stream("aa", [P, ROWS, PAD])
        cc = per_stream("cc", [P, ROWS, PAD])
        cv = per_stream("cv", [P, ROWS, PAD])
        sa = per_stream("sa", [P, ROWS, PAD])
        sbb = per_stream("sbb", [P, ROWS, PAD])
        num = per_stream("num", [P, ROWS, P])
        kf = per_stream("kf", [P, FF, N])
        stats = per_stream("stats", [P, ROWS, 6])
        mvar = per_stream("mvar", [P, ROWS, 2])
        veps = per_stream("veps", [P, ROWS])
        rstd = per_stream("rstd", [P, ROWS])
        msq = per_stream("msq", [P, ROWS])

        ctxs = per_stream("ctxs", [P, N])
        hi = per_stream("hi", [P, N], F32R)
        lo = per_stream("lo", [P, N], F32R)
        qs = per_stream("qs", [P, GROUPS, N], F32R)
        ks = per_stream("ks", [P, GROUPS, N], F32R)
        vext = per_stream("vext", [P, ROWS, HEADS, HEAD + 1])
        kbias = per_stream("kbias", [P, ROWS])
        brow = per_stream("brow", [P, N])
        bsp = per_stream("bsp", [P, N], F32R)
        smax = per_stream("smax", [P, 4, 32])
        mT = per_stream("mT", [P, P], F32R)
        rsum = per_stream("rsum", [P, HEADS])

        gt = per_stream("gt", [P, ROWS, EXPERTS])
        bi = per_stream("bi", [P, ROWS, EXPERTS])
        cmp1 = per_stream("cmp1", [P, ROWS, EXPERTS * EXPERTS])
        cmp2 = per_stream("cmp2", [P, ROWS, EXPERTS * EXPERTS])
        rank = per_stream("rank", [P, ROWS, EXPERTS])
        gmax = per_stream("gmax", [P, ROWS])
        wts = per_stream("wts", [P, ROWS, WROWS])
        whi = per_stream("whi", [P, ROWS, EXPERTS], F32R)

        ps = [ctx.enter_context(nc.psum_tensor(f"ps{s}", [P, 4, N], F32)) for s in range(STREAMS)]

        def inner(t):
            return t[:, :, 1:PAD]

        def before(t):
            return t[:, :, 0:P]

        def flat(t):
            return t[:, :, :].rearrange("p b t -> p (b t)")

        ee = den = dh
        zz = [inner(t) for t in pp]
        bhi = lo
        wT = [t[0:WROWS, :] for t in hi]
        xa = xn
        xT = mr
        probs = kf
        heads = dh
        oT = mk
        h_e = [[mk[s][:, :], dh[s][:, :, :].rearrange("p b t -> p (b t)")] for s in range(STREAMS)]
        silu_e = [[mv[s][:, :], num[s][:, :, :].rearrange("p b t -> p (b t)")] for s in range(STREAMS)]
        t_e = [[sr[s][:, :], kf[s][:, 0, :]] for s in range(STREAMS)]

        setup = {n: ctx.enter_context(nc.semaphore("set_" + n)) for n in
                 ("loads", "dup_loads", "pads", "consts", "own")}
        sig = {n: [ctx.enter_context(nc.semaphore(f"{n}{s}")) for s in range(STREAMS)] for n in SIGNALS}
        dve_own = [ctx.enter_context(nc.semaphore(f"dve_own{s}")) for s in range(STREAMS)]
        used = [q for pair in sig.values() for q in pair] + dve_own

        def slots():
            for k in range(2 * LAYERS + 1):
                time_mix = (k % 2, k // 2) if k < 2 * LAYERS else None
                channel_mix = ((k - 1) % 2, (k - 1) // 2) if k else None
                yield time_mix, channel_mix

        with nc.Block() as block:
            @block.sync
            def _(sp):
                sp.dma_start(VECS[:, :], vec).then_inc(setup["loads"], 16)
                sp.dma_start(CONST[:, :], const).then_inc(setup["loads"], 16)
                sp.dma_start(W[:, :, :], wl).then_inc(setup["loads"], 16)
                sp.dma_start(WX[:, :, :], wx).then_inc(setup["loads"], 16)
                sp.wait_ge(setup["loads"], 16 * 4)

            @block.scalar
            def _(act):
                for half in range(2):
                    act.dma_start(kf[half][:, 0:2, :].rearrange("p a b -> p (a b)"), dup[:, half, :]).then_inc(
                        setup["dup_loads"], 16)
                act.dma_start(WE[:, :, :], we).then_inc(setup["dup_loads"], 16)
                act.dma_start(WROUT[:, :], wrout).then_inc(setup["dup_loads"], 16)
                act.dma_start(ROWB[:, :], rows).then_inc(setup["dup_loads"], 16)
                act.dma_start(BDOWN[:, :], bdown).then_inc(setup["dup_loads"], 16)
                act.wait_ge(setup["loads"], 16 * 4)
                nc.scalar.activation(NEGW[:, :], VECS[:, VEC["decay"]:VEC["decay"] + LAYERS], ACT.Exp).then_inc(
                    setup["own"], 1)
                act.wait_ge(setup["dup_loads"], 16 * 6)

            @block.vector
            def _(dve):
                dve.wait_ge(setup["dup_loads"], 16 * 6)
                dve.wait_ge(setup["loads"], 16 * 4)
                for half in range(2):
                    nc.vector.tensor_copy(
                        DUP[:, 2 * GROUPS * half:2 * GROUPS * (half + 1), :].rearrange("p a b -> p (a b)"),
                        kf[half][:, 0:2, :].rearrange("p a b -> p (a b)"))
                nc.vector.tensor_copy(ONES2[:, :], CONST[:, P + 38:P + 39].broadcast_to([P, P]))
                nc.vector.tensor_copy(NEGEYE[:, :], CONST[:, P + 48:P + 48 + GROUPS])
                nc.vector.tensor_copy(WSEL[:, :], CONST[0:WROWS, P + 40:P + 40 + EXPERTS])
                nc.vector.memset(HALF[:, :], -0.5)
                nc.vector.tensor_scalar(ZTOP[:, :], VECS[:, VEC["first"]:VEC["first"] + LAYERS], -1.0, TOP,
                                        ALU.mult, ALU.add)
                for s in range(STREAMS):
                    nc.vector.memset(vext[s][:, :, :, HEAD:HEAD + 1], 1.0)
                    nc.vector.memset(wts[s][:, :, 2 * EXPERTS:WROWS], 1.0)
                dve.wait_ge(setup["own"], 1)
                dve.wait_ge(setup["pads"], 1)
                for l in range(LAYERS):
                    nc.vector.tensor_scalar(WPAD[:, l, :], WPAD[:, l, :], NEGW[:, l:l + 1], None,
                                            ALU.subtract).then_inc(setup["consts"], 1)
                dve.wait_ge(setup["consts"], LAYERS)
                wp = WPAD[:, :, :].rearrange("p l (b t) -> p (l b) t", t=PAD)
                nc.vector.memset(wp[:, :, 0:1], FAR)

            @block.gpsimd
            def _(pool):
                nc.gpsimd.memset(WPAD[:, :, :], 0.0).then_inc(setup["pads"], 1)
                for s in range(STREAMS):
                    nc.gpsimd.memset(hp[s][:, :, 0:1], 0.0)
                    nc.gpsimd.memset(kp[s][:, :, 0:1], FAR)
                    nc.gpsimd.memset(smax[s][:, :, :], 0.0)
                    for t in (aa, cc, cv):
                        nc.gpsimd.memset(t[s][:, :, 0:1], 0.0)

        with nc.Fori(0, PAIRS) as pair:
            with nc.Block() as block:
                both = range(STREAMS)

                @block.sync
                def _(sp):
                    for s in both:
                        first = pair * (STREAMS * ROWS) + s * ROWS
                        sp.dma_start(x0[s][:, :, :], xs[bass.ds(first, ROWS), :, :].rearrange("b t c -> t b c")
                                     ).then_inc(sig["x_loaded"][s], 16)
                    for s in both:
                        first = pair * (STREAMS * ROWS) + s * ROWS
                        sp.dma_start(ctxs[s][:, :], ctxT[:, bass.ds(first * P, N)]).then_inc(
                            sig["ctx_loaded"][s], 16)
                        sp.dma_start(brow[s][:, :], bias_rows[:, bass.ds(first * P, N)]).then_inc(
                            sig["bias_loaded"][s], 16)
                        sp.dma_start(kbias[s][:, :], biasT[:, bass.ds(first, ROWS)]).then_inc(
                            sig["bias_loaded"][s], 16)
                    for s in both:
                        first = pair * (STREAMS * ROWS) + s * ROWS
                        sp.wait_ge(sig["xn"][s], 2 * LAYERS + 4)
                        sp.dma_start(out[bass.ds(first, ROWS), :, :].rearrange("b t c -> t b c"), xn[s][:, :, :]
                                     ).then_inc(sig["stored"][s], 16)
                    for s in both:
                        sp.wait_ge(sig["stored"][s], 16)

                @block.gpsimd
                def _(pool):
                    norms = 1 + 2 * LAYERS + 2 + ROUNDS + 1
                    order = [0, 1, 0, 1]
                    for time_mix, channel_mix in slots():
                        order += [part[0] for part in (time_mix, channel_mix) if part]
                    order += [0, 1] * (norms - order.count(0))
                    seen = [0, 0]
                    for s in order:
                        seen[s] += 1
                        pool.wait_ge(sig["var"][s], seen[s])
                        nc.gpsimd.tensor_tensor(rstd[s][:, :], veps[s][:, :], HALF[:, :], ALU.pow).then_inc(
                            sig["rstd"][s], 1)

                @block.tensor
                def _(pe):
                    def transposes(s, src, bank):
                        for b in range(ROWS):
                            last = nc.tensor.transpose(ps[s][:, bank, b * P:(b + 1) * P], src[s][:, b, :], IDENT)
                        return last

                    def token_major(s, src, w, bank, first=True, stop=True):
                        for b in range(ROWS):
                            last = nc.tensor.matmul(ps[s][:, bank, b * P:(b + 1) * P], src[:, b * P:(b + 1) * P], w,
                                                    start=first and b == 0, stop=stop, skip_group_check=True)
                        return last

                    def product(s, w, src, bank, start=True, stop=True):
                        return nc.tensor.matmul(ps[s][:, bank, :], w, src, start=start, stop=stop)

                    def features(c, m, f):
                        product(c, W[:, LAYER_W * m + WCK + f, :], mk[c][:, :], f).then_inc(sig["kf"][c], 1)

                    def features_out(c, m, f):
                        pe.wait_ge(sig["squared"][c], FF * m + f + 1)
                        return token_major(c, kf[c][:, f, :], W[:, LAYER_W * m + WCV + f, :], 1, f == 0, f == FF - 1)

                    for time_mix, channel_mix in slots():
                        if channel_mix:
                            c, m = channel_mix
                            v = LAYER_W * m
                            pe.wait_ge(sig["xn"][c], 2 * m + 2)
                            transposes(c, xn, 0).then_inc(sig["xT"][c], 1)
                        if time_mix:
                            s, l = time_mix
                            w = LAYER_W * l
                            pe.wait_ge(sig["xn"][s], 2 * l + 1)
                            transposes(s, xn, 0).then_inc(sig["xT"][s], 1)
                        if channel_mix:
                            pe.wait_ge(sig["mixed2"][c], 2 * m + 1)
                            features(c, m, 0)
                            features(c, m, 1)
                        if time_mix:
                            pe.wait_ge(sig["mixed"][s], 3 * l + 1)
                            product(s, W[:, w + WK, :], mk[s][:, :], 1).then_inc(sig["k_ready"][s], 1)
                            pe.wait_ge(sig["mixed"][s], 3 * l + 2)
                            product(s, W[:, w + WV, :], mv[s][:, :], 2).then_inc(sig["v_ready"][s], 1)
                            pe.wait_ge(sig["mixed"][s], 3 * l + 3)
                            product(s, W[:, w + WR, :], mr[s][:, :], 3).then_inc(sig["r_ready"][s], 1)
                        if channel_mix:
                            features(c, m, 2)
                            features(c, m, 3)
                            pe.wait_ge(sig["mixed2"][c], 2 * m + 2)
                            pe.wait_ge(sig["relu"][c], FF * m + 1)
                            token_major(c, mr[c], W[:, v + WCR, :], 0).then_inc(sig["cr"][c], 1)
                            features_out(c, m, 0)
                            features_out(c, m, 1)
                        if time_mix:
                            pe.wait_ge(sig["rwkv"][s], l + 1)
                            token_major(s, num[s][:, :, :].rearrange("p b t -> p (b t)"), W[:, w + WO, :], 0).then_inc(
                                sig["wo"][s], 1)
                        if channel_mix:
                            features_out(c, m, 2)
                            features_out(c, m, 3).then_inc(sig["cv"][c], 1)

                    for s in both:
                        pe.wait_ge(sig["xn"][s], 2 * LAYERS + 1)
                        transposes(s, xn, 0).then_inc(sig["xT"][s], 1)
                    for s in both:
                        pe.wait_ge(sig["ctx_loaded"][s], 16)
                        product(s, WX[:, 1, :], ctxs[s][:, :], 2).then_inc(sig["kT"][s], 1)
                        token_major(s, ctxs[s], WX[:, 2, :], 3).then_inc(sig["vT"][s], 1)
                        pe.wait_ge(sig["h"][s], 2 * LAYERS + 1)
                        product(s, WX[:, 0, :], xT[s][:, :], 1).then_inc(sig["qT"][s], 1)
                    for which in range(2):
                        for s in both:
                            pe.wait_ge(sig["high"][s], which + 1)
                            pe.wait_ge(sig["low"][s], which + 1)
                            if which == 0:
                                pe.wait_ge(sig["vext"][s], 1)
                                pe.wait_ge(sig["k_kept"][s], 1)
                            for t in range(GROUPS):
                                if which == 1:
                                    pe.wait_ge(sig["dup_out"][s], t + 1)
                                at = 2 * GROUPS * which + t
                                nc.tensor.matmul(ps[s][:, t, :], DUP[:, at, :], hi[s][:, :], start=True, stop=False)
                                nc.tensor.matmul(ps[s][:, t, :], DUP[:, at + GROUPS, :], lo[s][:, :], start=False,
                                                 stop=True).then_inc(sig["dup"][s], 1)
                    for b in range(ROWS):
                        toks = slice(b * P, (b + 1) * P)
                        for s in both:
                            if b == 0:
                                pe.wait_ge(sig["dup_out"][s], 2 * GROUPS)
                                pe.wait_ge(sig["bias_split"][s], 1)
                            else:
                                pe.wait_ge(sig["heads_out"][s], b)
                            for g in range(4):
                                parts = slice(32 * g, 32 * g + 2)
                                bias = bsp[s][parts, toks].unsqueeze(1).broadcast_to([2, 4, P])
                                nc.tensor.matmul(ps[s][:, g, :].rearrange("p (t k) -> p t k", t=4), ONES2[parts, :], bias,
                                                 start=True, stop=False, skip_group_check=True)
                            for t in range(GROUPS):
                                for g in range(4):
                                    rows_ = slice(32 * g, 32 * g + 32)
                                    last = nc.tensor.matmul(ps[s][:, g, t * P:(t + 1) * P], qs[s][rows_, t, toks],
                                                            ks[s][rows_, t, toks], start=False, stop=t == GROUPS - 1,
                                                            skip_group_check=True)
                            last.then_inc(sig["s_ready"][s], 1)
                        for s in both:
                            pe.wait_ge(sig["s_max"][s], b + 1)
                            nc.tensor.transpose(ps[s][:, 0, 0:P], smax[s][:, :, :].rearrange("p g t -> p (g t)"), IDENT).then_inc(sig["mT"][s], 1)
                        for s in both:
                            pe.wait_ge(sig["mT_out"][s], b + 1)
                            for g in range(4):
                                for t in range(GROUPS):
                                    rows_ = slice(32 * g, 32 * g + GROUPS)
                                    nc.tensor.matmul(ps[s][:, g, t * P:(t + 1) * P],
                                                     NEGEYE[rows_, t:t + 1].broadcast_to([GROUPS, P]),
                                                     mT[s][rows_, :], start=t == 0, stop=False, skip_group_check=True)
                            for t in range(GROUPS):
                                for g in range(4):
                                    rows_ = slice(32 * g, 32 * g + 32)
                                    last = nc.tensor.matmul(ps[s][:, g, t * P:(t + 1) * P], ks[s][rows_, t, toks],
                                                            qs[s][rows_, t, toks], start=False, stop=t == GROUPS - 1,
                                                            skip_group_check=True)
                            last.then_inc(sig["st_ready"][s], 1)
                        for s in both:
                            pe.wait_ge(sig["probs"][s], b + 1)
                            for g in range(4):
                                for t in range(GROUPS):
                                    h = 4 * t + g
                                    last = nc.tensor.matmul(
                                        ps[s][:, 0, h * (HEAD + 1):(h + 1) * (HEAD + 1)],
                                        probs[s][:, g, t * P:(t + 1) * P], vext[s][:, b, h, :],
                                        start=g == 0 and t == 0, stop=True, skip_group_check=True)
                            last.then_inc(sig["pv"][s], 1)
                    for s in both:
                        pe.wait_ge(sig["heads_out"][s], ROWS)
                        transposes(s, heads, 0).then_inc(sig["oT"][s], 1)
                    for s in both:
                        pe.wait_ge(sig["oT_out"][s], 1)
                        token_major(s, oT[s], WX[:, 3, :], 1).then_inc(sig["attn"][s], 1)

                    for j in range(ROUNDS):
                        for s in both:
                            if j == 0:
                                pe.wait_ge(sig["xn"][s], 2 * LAYERS + 2)
                            else:
                                pe.wait_ge(sig["x_new"][s], j)
                            transposes(s, x if j else xn, 0).then_inc(sig["xT"][s], 1)
                        for s in both:
                            pe.wait_ge(sig["h"][s], 2 * LAYERS + 2 + j)
                            for b in range(ROWS):
                                last = nc.tensor.matmul(ps[s][:, 2, b * EXPERTS:(b + 1) * EXPERTS],
                                                        xT[s][:, b * P:(b + 1) * P],
                                                        WROUT[:, j * EXPERTS:(j + 1) * EXPERTS],
                                                        start=b == 0, stop=True, skip_group_check=True)
                            last.then_inc(sig["gate"][s], 1)
                        for s in both:
                            product(s, WE[:, 0, :], xT[s][:, :], 0).then_inc(sig["up"][s], 1)
                        for u in range(UNITS):
                            n = UNITS * j + u
                            for s in both:
                                pe.wait_ge(sig["h_out"][s], n + 1)
                                if n:
                                    pe.wait_ge(sig["silu"][s], n)
                                product(s, WE[:, UNITS + u, :], h_e[s][u % 2], 1).then_inc(sig["g_ready"][s], 1)
                            if u < UNITS - 1:
                                for s in both:
                                    product(s, WE[:, u + 1, :], xT[s][:, :], 0).then_inc(sig["up"][s], 1)
                            if u == SHARED:
                                for s in both:
                                    pe.wait_ge(sig["w_split"][s], j + 1)
                                    for b in range(ROWS):
                                        last = nc.tensor.transpose(ps[s][0:WROWS, 2, b * P:(b + 1) * P], wts[s][:, b, :],
                                                                   IDENT)
                                    last.then_inc(sig["wT"][s], 1)
                            if u >= SHARED:
                                for s in both:
                                    if u == SHARED:
                                        pe.wait_ge(sig["wT_out"][s], j + 1)
                                    else:
                                        pe.wait_ge(sig["t_out"][s], n)
                                    product(s, WSEL[:, u - SHARED:u - SHARED + 1].broadcast_to([WROWS, P]), wT[s][:, :],
                                            2).then_inc(sig["wb"][s], 1)
                            for s in both:
                                pe.wait_ge(sig["t_out"][s], n + 1)
                                token_major(s, t_e[s][u % 2], WE[:, 2 * UNITS + u, :], 3, u == 0, False).then_inc(
                                    sig["z_part"][s], 1)
                        for s in both:
                            for b in range(ROWS):
                                last = nc.tensor.matmul(ps[s][:, 3, b * P:(b + 1) * P],
                                                        wT[s][:, b * P:(b + 1) * P].bitcast(F32), BDOWN[:, :],
                                                        start=False, stop=True, skip_group_check=True)
                            last.then_inc(sig["z_done"][s], 1)

                @block.scalar
                def _(act):
                    def vecs(name, l):
                        return VECS[:, VEC[name] + l:VEC[name] + l + 1]

                    def normed_h(s, l, half):
                        act.wait_ge(sig["xT"][s], 2 * l + half)
                        nc.scalar.activation(inner(hp[s]), ps[s][:, 0, :].rearrange("p (b t) -> p b t", t=P),
                                             ACT.Identity, scale=vecs(f"ln{half}_w", l),
                                             bias=vecs(f"ln{half}_b", l)).then_inc(sig["h"][s], 1)

                    def relu(c, m, f):
                        act.wait_ge(sig["kf"][c], FF * m + f + 1)
                        nc.scalar.activation(kf[c][:, f, :], ps[c][:, f, :], ACT.Relu).then_inc(sig["relu"][c], 1)

                    def square(c, m, f):
                        act.wait_ge(sig["relu"][c], FF * m + f + 1)
                        nc.scalar.activation(kf[c][:, f, :], kf[c][:, f, :], ACT.Square).then_inc(
                            sig["squared"][c], 1)

                    for time_mix, channel_mix in slots():
                        if channel_mix:
                            c, m = channel_mix
                            normed_h(c, m, 2)
                        if time_mix:
                            s, l = time_mix
                            normed_h(s, l, 1)
                        if time_mix:
                            if channel_mix:
                                relu(c, m, 0)
                                relu(c, m, 1)
                            act.wait_ge(sig["k_ready"][s], l + 1)
                            nc.scalar.activation(inner(kp[s]), ps[s][:, 1, :].rearrange("p (b t) -> p b t", t=P),
                                                 ACT.Identity).then_inc(sig["kp"][s], 1)
                            act.wait_ge(sig["r_ready"][s], l + 1)
                            nc.scalar.activation(sr[s][:, :], ps[s][:, 3, :], ACT.Sigmoid).then_inc(sig["sr"][s], 1)
                        elif channel_mix:
                            relu(c, m, 0)
                            relu(c, m, 1)
                        if time_mix:
                            nc.scalar.preload_act_table_set("natural_log_exp_and_others")
                            act.wait_ge(sig["args"][s], 3 * l + 1)
                            nc.scalar.activation(inner(cc[s]), inner(cc[s]), ACT.Exp).then_inc(sig["decays"][s], 1)
                            act.wait_ge(sig["args"][s], 3 * l + 2)
                            nc.scalar.activation(inner(aa[s]), inner(aa[s]), ACT.Exp, scale=-1.0).then_inc(
                                sig["decays"][s], 1)
                            act.wait_ge(sig["args"][s], 3 * l + 3)
                            nc.scalar.activation(zz[s], zz[s], ACT.Exp, bias=vecs("first", l)).then_inc(
                                sig["decays"][s], 1)
                        if channel_mix:
                            relu(c, m, 2)
                            relu(c, m, 3)
                            square(c, m, 0)
                            square(c, m, 1)
                        if time_mix:
                            act.wait_ge(sig["den"][s], l + 1)
                            nc.scalar.activation(den[s][:, :, :], den[s][:, :, :], ACT.Ln).then_inc(
                                sig["act_own"][s], 1)
                            act.wait_ge(sig["act_own"][s], l + 1)
                            nc.scalar.activation(den[s][:, :, :], den[s][:, :, :], ACT.Exp, scale=-1.0).then_inc(
                                sig["inv"][s], 1)
                        if channel_mix:
                            square(c, m, 2)
                            square(c, m, 3)
                            act.wait_ge(sig["cr"][c], m + 1)
                            nc.scalar.activation(sr[c][:, :], ps[c][:, 0, :], ACT.Sigmoid).then_inc(sig["sig"][c], 1)

                    for s in both:
                        act.wait_ge(sig["xT"][s], 2 * LAYERS + 1)
                        nc.scalar.activation(xT[s][:, :], ps[s][:, 0, :], ACT.Identity).then_inc(sig["h"][s], 1)
                    for s in both:
                        act.wait_ge(sig["vT"][s], 1)
                        nc.scalar.activation(vext[s][:, :, :, 0:HEAD],
                                             ps[s][:, 3, :].rearrange("p (b h d) -> p b h d", b=ROWS, d=HEAD),
                                             ACT.Identity).then_inc(sig["vext"][s], 1)
                    for which in range(2):
                        for s in both:
                            if which == 0:
                                act.wait_ge(sig["qT"][s], 1)
                            else:
                                act.wait_ge(sig["low"][s], 1)
                                act.wait_ge(sig["k_kept"][s], 1)
                                act.wait_ge(sig["dup"][s], GROUPS)
                            source = ps[s][:, 1, :] if which == 0 else mv[s][:, :]
                            nc.scalar.activation(hi[s][:, :], source, ACT.Identity).then_inc(sig["high"][s], 1)
                            if which == 0:
                                act.wait_ge(sig["kT"][s], 1)
                                nc.scalar.activation(mv[s][:, :], ps[s][:, 2, :], ACT.Identity).then_inc(
                                    sig["k_kept"][s], 1)
                        for s in both:
                            dst = ks if which else qs
                            for t in range(GROUPS):
                                act.wait_ge(sig["dup"][s], GROUPS * which + t + 1)
                                nc.scalar.activation(dst[s][:, t, :], ps[s][:, t, :], ACT.Identity).then_inc(
                                    sig["dup_out"][s], 1)
                    for b in range(ROWS):
                        for s in both:
                            act.wait_ge(sig["mT"][s], b + 1)
                            nc.scalar.activation(mT[s][:, :], ps[s][:, 0, 0:P], ACT.Identity).then_inc(
                                sig["mT_out"][s], 1)
                        for s in both:
                            act.wait_ge(sig["st_ready"][s], b + 1)
                            act.wait_ge(sig["bias_loaded"][s], 32)
                            if b:
                                act.wait_ge(sig["pv"][s], b)
                            nc.scalar.activation(probs[s][:, :, :].rearrange("p a b -> p (a b)"),
                                                 ps[s][:, :, :].rearrange("p a b -> p (a b)"), ACT.Exp,
                                                 bias=kbias[s][:, b:b + 1], scale=HEAD ** -0.5).then_inc(
                                sig["probs"][s], 1)
                    for s in both:
                        act.wait_ge(sig["oT"][s], 1)
                        nc.scalar.activation(oT[s][:, :], ps[s][:, 0, :], ACT.Identity).then_inc(sig["oT_out"][s], 1)

                    for j in range(ROUNDS):
                        for s in both:
                            act.wait_ge(sig["xT"][s], 2 * LAYERS + 2 + j)
                            nc.scalar.activation(xT[s][:, :], ps[s][:, 0, :], ACT.Identity).then_inc(sig["h"][s], 1)
                        def up_out(u):
                            n = UNITS * j + u
                            at = VEC_SBUP + u if u < SHARED else VEC_BUP + u - SHARED
                            for s in both:
                                act.wait_ge(sig["up"][s], n + 1)
                                if n > 1:
                                    act.wait_ge(sig["t_out"][s], n - 1)
                                nc.scalar.activation(h_e[s][u % 2], ps[s][:, 0, :], ACT.Identity,
                                                     bias=VECS[:, at:at + 1]).then_inc(sig["h_out"][s], 1)

                        up_out(0)
                        for u in range(UNITS):
                            n = UNITS * j + u
                            if u == 0:
                                for s in both:
                                    act.wait_ge(sig["gate_max"][s], j + 1)
                                    nc.scalar.activation(gt[s][:, :, :], gt[s][:, :, :], ACT.Exp).then_inc(
                                        sig["gate_exp"][s], 1)
                            at = VEC_SBG if u < SHARED else VEC_BG + u - SHARED
                            for s in both:
                                act.wait_ge(sig["g_ready"][s], n + 1)
                                nc.scalar.activation(silu_e[s][u % 2], ps[s][:, 1, :], ACT.Silu,
                                                     bias=VECS[:, at:at + 1]).then_inc(sig["silu"][s], 1)
                            if u < UNITS - 1:
                                up_out(u + 1)
                            if u == SHARED:
                                for s in both:
                                    act.wait_ge(sig["wT"][s], j + 1)
                                    nc.scalar.activation(wT[s], ps[s][0:WROWS, 2, :], ACT.Identity).then_inc(
                                        sig["wT_out"][s], 1)

                @block.vector
                def _(dve):
                    steps = [0, 0]
                    norms = [0, 0]
                    halves = [0, 0]

                    def done(s, ins):
                        ins.then_inc(dve_own[s], 1)
                        steps[s] += 1
                        return steps[s]

                    def need(s, n):
                        dve.wait_ge(dve_own[s], n)

                    def variances(s, src, eps, rms=False):
                        for b in range(ROWS):
                            n = done(s, nc.vector.bn_stats(stats[s][:, b, :], src[s][:, b, :]))
                        need(s, n)
                        for b in range(ROWS):
                            n = done(s, nc.vector.bn_aggr(mvar[s][:, b, :], stats[s][:, b, :]))
                        need(s, n)
                        if rms:
                            n = done(s, nc.vector.tensor_tensor(msq[s][:, :], mvar[s][:, :, 0], mvar[s][:, :, 0],
                                                                ALU.mult))
                            need(s, n)
                            nc.vector.scalar_tensor_tensor(veps[s][:, :], msq[s][:, :], eps, mvar[s][:, :, 1],
                                                           ALU.add, ALU.add).then_inc(sig["var"][s], 1)
                        else:
                            nc.vector.tensor_scalar(veps[s][:, :], mvar[s][:, :, 1], eps, None, ALU.add).then_inc(
                                sig["var"][s], 1)

                    def normed(s, dst, src):
                        norms[s] += 1
                        dve.wait_ge(sig["rstd"][s], norms[s])
                        for b in range(ROWS):
                            last = nc.vector.tensor_scalar(dst[s][:, b, :], src[s][:, b, :], mvar[s][:, b, 0:1],
                                                           rstd[s][:, b:b + 1], ALU.subtract, ALU.mult)
                        return last

                    for s in both:
                        dve.wait_ge(sig["x_loaded"][s], 16)
                        variances(s, x0, EPS)
                    for s in both:
                        need(s, done(s, normed(s, x, x0)))
                        row = ROWB[:, ROW_LN0W:ROW_LN0W + P].unsqueeze(1).broadcast_to([P, ROWS, P])
                        need(s, done(s, nc.vector.tensor_tensor(x[s][:, :, :], x[s][:, :, :], row, ALU.mult)))
                        row = ROWB[:, ROW_LN0B:ROW_LN0B + P].unsqueeze(1).broadcast_to([P, ROWS, P])
                        need(s, done(s, nc.vector.tensor_tensor(x[s][:, :, :], x[s][:, :, :], row, ALU.add)))
                        variances(s, x, EPS)

                    def vecs(name, l):
                        return VECS[:, VEC[name] + l:VEC[name] + l + 1]

                    def back(s, l, n):
                        dve.wait_ge(sig["h"][s], 2 * l + n)
                        need(s, done(s, nc.vector.tensor_tensor(dh[s][:, :, :], inner(hp[s]), before(hp[s]),
                                                                ALU.subtract)))

                    def mix(s, l, dst, name):
                        return nc.vector.scalar_tensor_tensor(
                            dst[s][:, :].rearrange("p (b t) -> p b t", t=P), dh[s][:, :, :], vecs(name, l),
                            before(hp[s]), ALU.mult, ALU.add)

                    for time_mix, channel_mix in slots():
                        if channel_mix:
                            c, m = channel_mix
                            normed(c, xn, x).then_inc(sig["xn"][c], 1)
                        if time_mix:
                            s, l = time_mix
                            normed(s, xn, x).then_inc(sig["xn"][s], 1)
                        if channel_mix:
                            back(c, m, 2)
                            mix(c, m, mk, "cmk").then_inc(sig["mixed2"][c], 1)
                        if time_mix:
                            back(s, l, 1)
                            mix(s, l, mk, "tmk").then_inc(sig["mixed"][s], 1)
                            mix(s, l, mv, "tmv").then_inc(sig["mixed"][s], 1)
                            mix(s, l, mr, "tmr").then_inc(sig["mixed"][s], 1)
                        if channel_mix:
                            mix(c, m, mr, "cmr").then_inc(sig["mixed2"][c], 1)
                        if time_mix:
                            dve.wait_ge(sig["kp"][s], l + 1)
                            need(s, done(s, nc.vector.tensor_tensor_scan(flat(pp[s]), WPAD[:, l, :], flat(kp[s]), FAR,
                                                                         ALU.add, ALU.max)))
                            need(s, done(s, nc.vector.tensor_tensor(ee[s][:, :, :], inner(kp[s]), before(pp[s]),
                                                                    ALU.subtract)))
                            nc.vector.tensor_scalar(inner(cc[s]), ee[s][:, :, :], NEGW[:, l:l + 1], 0.0, ALU.add,
                                                    ALU.min).then_inc(sig["args"][s], 1)
                            nc.vector.tensor_scalar(inner(aa[s]), ee[s][:, :, :], NEGW[:, l:l + 1], 0.0, ALU.add,
                                                    ALU.max).then_inc(sig["args"][s], 1)
                            nc.vector.tensor_scalar(zz[s], ee[s][:, :, :], ZTOP[:, l:l + 1], None,
                                                    ALU.min).then_inc(sig["args"][s], 1)
                            v = ps[s][:, 2, :].rearrange("p (b t) -> p b t", t=P)
                            dve.wait_ge(sig["v_ready"][s], l + 1)
                            dve.wait_ge(sig["decays"][s], 3 * l + 1)
                            n_cv = done(s, nc.vector.tensor_tensor(inner(cv[s]), inner(cc[s]), v, ALU.mult))
                            dve.wait_ge(sig["decays"][s], 3 * l + 2)
                            n_b = done(s, nc.vector.tensor_tensor_scan(flat(sbb[s]), flat(aa[s]), flat(cc[s]), 0.0,
                                                                       ALU.mult, ALU.add))
                            dve.wait_ge(sig["decays"][s], 3 * l + 3)
                            n_zv = done(s, nc.vector.tensor_tensor(num[s][:, :, :], zz[s], v, ALU.mult))
                            need(s, n_b)
                            nc.vector.tensor_tensor(den[s][:, :, :], zz[s], before(sbb[s]), ALU.add).then_inc(
                                sig["den"][s], 1)
                            need(s, n_cv)
                            n_a = done(s, nc.vector.tensor_tensor_scan(flat(sa[s]), flat(aa[s]), flat(cv[s]), 0.0,
                                                                       ALU.mult, ALU.add))
                            need(s, n_a)
                            need(s, done(s, nc.vector.tensor_tensor(num[s][:, :, :], num[s][:, :, :], before(sa[s]),
                                                                    ALU.add)))
                            dve.wait_ge(sig["sr"][s], l + 1)
                            n_sr = done(s, nc.vector.tensor_tensor(
                                num[s][:, :, :], num[s][:, :, :], sr[s][:, :].rearrange("p (b t) -> p b t", t=P),
                                ALU.mult))
                            dve.wait_ge(sig["inv"][s], l + 1)
                            need(s, n_sr)
                            nc.vector.tensor_tensor(num[s][:, :, :], num[s][:, :, :], den[s][:, :, :],
                                                    ALU.mult).then_inc(sig["rwkv"][s], 1)
                        if time_mix:
                            dve.wait_ge(sig["wo"][s], l + 1)
                            need(s, done(s, nc.vector.tensor_tensor(
                                x[s][:, :, :], x[s][:, :, :], ps[s][:, 0, :].rearrange("p (b t) -> p b t", t=P),
                                ALU.add)))
                            variances(s, x, EPS)
                        if channel_mix:
                            dve.wait_ge(sig["sig"][c], m + 1)
                            dve.wait_ge(sig["cv"][c], m + 1)
                            need(c, done(c, nc.vector.tensor_tensor(sr[c][:, :], sr[c][:, :], ps[c][:, 1, :],
                                                                    ALU.mult)))
                            need(c, done(c, nc.vector.tensor_tensor(
                                x[c][:, :, :], x[c][:, :, :], sr[c][:, :].rearrange("p (b t) -> p b t", t=P), ALU.add)))
                            if m == LAYERS - 1:
                                need(c, done(c, nc.vector.tensor_tensor(x[c][:, :, :], x[c][:, :, :], x0[c][:, :, :],
                                                                        ALU.add)))
                            variances(c, x, EPS)

                    for s in both:
                        normed(s, xa, x).then_inc(sig["xn"][s], 1)
                    for s in both:
                        dve.wait_ge(sig["bias_loaded"][s], 32)
                        need(s, done(s, nc.vector.tensor_scalar(brow[s][:, :], brow[s][:, :], HEAD ** 0.5, None,
                                                                ALU.mult)))
                        need(s, done(s, nc.vector.tensor_copy(bhi[s][:, :], brow[s][:, :])))
                        need(s, done(s, nc.vector.tensor_scalar(bhi[s][:, :], bhi[s][:, :].bitcast(F32), PART, None,
                                                                ALU.mult)))
                        nc.vector.tensor_tensor(bsp[s][:, :], brow[s][:, :], bhi[s][:, :].bitcast(F32),
                                                ALU.subtract).then_inc(sig["bias_split"][s], 1)
                    for which in range(2):
                        for s in both:
                            dve.wait_ge(sig["high"][s], which + 1)
                            if which == 1:
                                dve.wait_ge(sig["dup"][s], GROUPS)
                            else:
                                dve.wait_ge(sig["bias_split"][s], 1)
                            source = ps[s][:, 1, :] if which == 0 else mv[s][:, :]
                            nc.vector.tensor_tensor(lo[s][:, :], source, hi[s][:, :].bitcast(F32),
                                                    ALU.subtract).then_inc(sig["low"][s], 1)
                    for b in range(ROWS):
                        for s in both:
                            dve.wait_ge(sig["s_ready"][s], b + 1)
                            nc.vector.tensor_reduce(smax[s][:, :, 0:GROUPS],
                                                    ps[s][:, :, :].rearrange("p g (t k) -> p g t k", k=P),
                                                    AX.X, ALU.max).then_inc(sig["s_max"][s], 1)
                        for s in both:
                            dve.wait_ge(sig["pv"][s], b + 1)
                            o = ps[s][:, 0, 0:HEADS * (HEAD + 1)].rearrange("p (h d) -> p h d", d=HEAD + 1)
                            need(s, done(s, nc.vector.reciprocal(rsum[s][:, :], o[:, :, HEAD])))
                            nc.vector.tensor_tensor(heads[s][:, b, :].rearrange("p (h d) -> p h d", d=HEAD),
                                                    o[:, :, 0:HEAD],
                                                    rsum[s][:, :].unsqueeze(2).broadcast_to([P, HEADS, HEAD]),
                                                    ALU.mult).then_inc(sig["heads_out"][s], 1)
                    for s in both:
                        dve.wait_ge(sig["attn"][s], 1)
                        need(s, done(s, nc.vector.tensor_tensor(
                            x[s][:, :, :], xa[s][:, :, :], ps[s][:, 1, :].rearrange("p (b t) -> p b t", t=P), ALU.add)))
                        variances(s, x, EPS)
                    for s in both:
                        normed(s, xa, x).then_inc(sig["xn"][s], 1)

                    for j in range(ROUNDS):
                        rb = ROWB[:, ROW_RB + j * EXPERTS:ROW_RB + (j + 1) * EXPERTS].unsqueeze(1).broadcast_to(
                            [P, ROWS, EXPERTS])
                        gb = ROWB[:, ROW_GB + j * EXPERTS:ROW_GB + (j + 1) * EXPERTS].unsqueeze(1).broadcast_to(
                            [P, ROWS, EXPERTS])
                        for s in both:
                            dve.wait_ge(sig["gate"][s], j + 1)
                            need(s, done(s, nc.vector.tensor_tensor(
                                gt[s][:, :, :], ps[s][:, 2, 0:ROWS * EXPERTS].rearrange("p (b e) -> p b e", e=EXPERTS),
                                rb, ALU.add)))
                            need(s, done(s, nc.vector.tensor_tensor(bi[s][:, :, :], gt[s][:, :, :], gb, ALU.add)))
                            for b in range(ROWS):
                                shape = [P, EXPERTS, EXPERTS]
                                other = bi[s][:, b, :].unsqueeze(1).broadcast_to(shape)
                                own = bi[s][:, b, :].unsqueeze(2).broadcast_to(shape)
                                c1 = cmp1[s][:, b, :].rearrange("p (e f) -> p e f", f=EXPERTS)
                                c2 = cmp2[s][:, b, :].rearrange("p (e f) -> p e f", f=EXPERTS)
                                done(s, nc.vector.tensor_tensor(c1, other, own, ALU.is_gt))
                                n = done(s, nc.vector.tensor_tensor(c2, other, own, ALU.is_equal))
                            need(s, n)
                            lower = LOWER.unsqueeze(1).broadcast_to([P, ROWS, EXPERTS * EXPERTS])
                            need(s, done(s, nc.vector.tensor_tensor(cmp2[s][:, :, :], cmp2[s][:, :, :], lower,
                                                                    ALU.mult)))
                            need(s, done(s, nc.vector.tensor_tensor(cmp1[s][:, :, :], cmp1[s][:, :, :],
                                                                    cmp2[s][:, :, :], ALU.add)))
                            need(s, done(s, nc.vector.tensor_reduce(
                                rank[s][:, :, :].rearrange("p b e -> p (b e)"),
                                cmp1[s][:, :, :].rearrange("p b (e f) -> p (b e) f", f=EXPERTS), AX.X, ALU.add)))
                            need(s, done(s, nc.vector.tensor_scalar(rank[s][:, :, :], rank[s][:, :, :], 1.5, -1e30,
                                                                    ALU.is_gt, ALU.mult)))
                            need(s, done(s, nc.vector.tensor_tensor(gt[s][:, :, :], gt[s][:, :, :], rank[s][:, :, :],
                                                                    ALU.add)))
                            need(s, done(s, nc.vector.tensor_reduce(gmax[s][:, :], gt[s][:, :, :], AX.X, ALU.max)))
                            nc.vector.tensor_tensor(gt[s][:, :, :], gt[s][:, :, :],
                                                    gmax[s][:, :].unsqueeze(2).broadcast_to([P, ROWS, EXPERTS]),
                                                    ALU.subtract).then_inc(sig["gate_max"][s], 1)
                        for s in both:
                            dve.wait_ge(sig["gate_exp"][s], j + 1)
                            need(s, done(s, nc.vector.tensor_reduce(gmax[s][:, :], gt[s][:, :, :], AX.X, ALU.add)))
                            need(s, done(s, nc.vector.reciprocal(gmax[s][:, :], gmax[s][:, :])))
                            need(s, done(s, nc.vector.tensor_tensor(
                                gt[s][:, :, :], gt[s][:, :, :],
                                gmax[s][:, :].unsqueeze(2).broadcast_to([P, ROWS, EXPERTS]), ALU.mult)))
                            need(s, done(s, nc.vector.tensor_copy(whi[s][:, :, :], gt[s][:, :, :])))
                            n1 = done(s, nc.vector.tensor_copy(wts[s][:, :, 0:EXPERTS], whi[s][:, :, :].bitcast(F32)))
                            need(s, n1)
                            nc.vector.tensor_tensor(wts[s][:, :, EXPERTS:2 * EXPERTS], gt[s][:, :, :],
                                                    whi[s][:, :, :].bitcast(F32), ALU.subtract).then_inc(
                                sig["w_split"][s], 1)
                        for u in range(UNITS):
                            n = UNITS * j + u
                            for s in both:
                                dve.wait_ge(sig["silu"][s], n + 1)
                                if n > 1:
                                    dve.wait_ge(sig["z_part"][s], n - 1)
                                mul = nc.vector.tensor_tensor(t_e[s][u % 2], silu_e[s][u % 2], h_e[s][u % 2], ALU.mult)
                                if u < SHARED:
                                    mul.then_inc(sig["t_out"][s], 1)
                                else:
                                    halves[s] = done(s, mul)
                            if u >= SHARED:
                                for s in both:
                                    need(s, halves[s])
                                    dve.wait_ge(sig["wb"][s], EXPERTS * j + u - SHARED + 1)
                                    nc.vector.tensor_tensor(t_e[s][u % 2], t_e[s][u % 2], ps[s][:, 2, :],
                                                            ALU.mult).then_inc(sig["t_out"][s], 1)
                        for s in both:
                            src = x if j else xa
                            dve.wait_ge(sig["z_done"][s], j + 1)
                            need(s, done(s, nc.vector.tensor_tensor(
                                x[s][:, :, :], src[s][:, :, :], ps[s][:, 3, :].rearrange("p (b t) -> p b t", t=P),
                                ALU.add)))
                            variances(s, x, RMS_EPS, rms=True)
                        for s in both:
                            norms[s] += 1
                            dve.wait_ge(sig["rstd"][s], norms[s])
                            for b in range(ROWS):
                                last = nc.vector.scalar_tensor_tensor(
                                    x[s][:, b, :], x[s][:, b, :], rstd[s][:, b:b + 1],
                                    ROWB[:, ROW_NORM + j * P:ROW_NORM + (j + 1) * P], ALU.mult, ALU.mult)
                            last.then_inc(sig["x_new"][s], 1)
                    for s in both:
                        dve.wait_ge(sig["x_new"][s], ROUNDS)
                        need(s, done(s, nc.vector.tensor_tensor(x[s][:, :, :], x[s][:, :, :], xa[s][:, :, :],
                                                                ALU.add)))
                        variances(s, x, EPS)
                    for s in both:
                        normed(s, xn, x).then_inc(sig["xn"][s], 2)
            nc.all_engine_barrier(sems_to_clear=range(used[0].num, used[-1].num + 1))


def kernel(**inputs):
    import numpy as np
    import concourse.bacc as bacc
    from concourse import mybir as mb
    from concourse.bass_utils import run_bass_kernel_spmd

    a = {k: np.asarray(v) for k, v in inputs.items()}
    r = {k[8:]: v for k, v in a.items() if k.startswith("L0_attn_")}
    t = {k[9:]: v for k, v in a.items() if k.startswith("L0_xattn_")}
    f = {k[7:]: v for k, v in a.items() if k.startswith("L0_ffn_")}

    def chunks(w):
        return [w[:, i:i + P] for i in range(0, w.shape[1], P)]

    wl = []
    for l in range(LAYERS):
        wl += [r[n][l].T for n in ("Wr", "Wk", "Wv", "Wo")] + [r["Wcr"][l].T] + chunks(r["Wck"][l].T)
        wl += [r["Wcv"][l].T[i:i + P] for i in range(0, FF * P, P)]
    wx = [t[n].T for n in ("Wq", "Wk", "Wv", "Wo")]
    we = chunks(f["share_Wup"]) + list(f["exp_Wup"]) + [f["share_Wg"]] * SHARED + list(f["exp_Wg"])
    we += [f["share_Wdown"]] * SHARED + list(f["exp_Wdown"])
    vec = [r[n].T for n in ("ln1_w", "ln1_b", "ln2_w", "ln2_b", "time_decay", "time_first", "tmk", "tmv", "tmr",
                            "cmk", "cmr")]
    vec += [f["exp_bup"].T, f["share_bup"].reshape(SHARED, P).T, f["exp_bg"].T, f["share_bg"].reshape(1, P).T]
    rows = np.concatenate([r["ln0_w"], r["ln0_b"], f["norm_w"].ravel(), f["router_b"].ravel(), f["gate_bias"].ravel()])
    bdown = np.concatenate([f["exp_bdown"], f["exp_bdown"], np.stack([f["share_bdown"]] * SHARED)])

    const = np.zeros((P, P + 64), np.float32)
    const[:, :P] = np.eye(P)
    const[:, P:P + 36] = np.tri(EXPERTS, k=-1).reshape(1, 36)
    const[1::2, P + 36] = 1.0
    const[:, P + 38] = 1.0
    for g in range(4):
        const[range(32 * g, 32 * g + GROUPS), range(P + 48, P + 48 + GROUPS)] = -1.0
    for e in range(EXPERTS):
        const[[e, EXPERTS + e], P + 40 + e] = 1.0
    dup = np.zeros((P, 2, 2, GROUPS, P), np.float32)
    for which, highs in enumerate(((0, 2), (0, 1))):
        for g in range(GROUPS):
            for place in range(4):
                for part in range(4):
                    for d in range(HEAD):
                        dup[HEAD * (4 * g + place) + d, which, int(part not in highs), g, 32 * place + 8 * part + d] = 1

    arrays = {
        "xs": a["x"],
        "ctxT": a["ctx_1024"].reshape(-1, P).T,
        "biasT": a["fside_BxS2_0"].T,
        "bias_rows": np.broadcast_to(a["fside_BxS2_0"].reshape(1, -1), (P, a["fside_BxS2_0"].size)),
        "wl": np.stack(wl, 1), "wx": np.stack(wx, 1), "we": np.stack(we, 1),
        "wrout": np.concatenate(list(f["router_W"]), 1),
        "vec": np.concatenate(vec, 1), "rows": np.broadcast_to(rows, (P, ROW_N)), "bdown": bdown,
        "const": const, "dup": dup.reshape(P, 2, 2 * GROUPS * P),
    }
    nc = bacc.Bacc("TRN2", target_bir_lowering=False, num_devices=1)
    arrays = {n: np.ascontiguousarray(v) for n, v in arrays.items()}
    args = [nc.dram_tensor(n, v.shape, mb.dt.from_np(v.dtype), kind="ExternalInput").ap() for n, v in arrays.items()]
    out = nc.dram_tensor("out", a["x"].shape, F32, kind="ExternalOutput").ap()
    network(nc, *args, out)
    result = run_bass_kernel_spmd(nc, [arrays], core_ids=[0])
    return result.results[0]["out"]
```

```python
from contextlib import ExitStack

import concourse.bass as bass
from concourse import mybir

P = 128
LAYERS = 4
ROWS = 4
N = ROWS * P
PAD = P + 1
STREAMS = 2
HEADS = 16
HEAD = P // HEADS
GROUPS = HEADS // 4
DIAG = 4 * 64 + HEAD
EXPERTS = 6
SHARED = 2
ROUNDS = 2
FF = 4
EPS = 1e-5
RMS_EPS = 1e-6
FAR = -1e38
TOP = 40.0

F32 = mybir.dt.float32
F32R = mybir.dt.float32r
ALU = mybir.AluOpType
ACT = mybir.ActivationFunctionType
AX = mybir.AxisListType

VEC = {name: 4 * n for n, name in enumerate(
    ["ln1_w", "ln1_b", "ln2_w", "ln2_b", "decay", "first", "tmk", "tmv", "tmr", "cmk", "cmr"])}
VEC_BUP, VEC_SBUP, VEC_BG, VEC_SBG, VEC_N = 44, 50, 52, 58, 59
WR, WK, WV, WO, WCR, WCK, WCV, LAYER_W = 0, 1, 2, 3, 4, 5, 9, 13
UNITS = SHARED + EXPERTS
ROW_LN0W, ROW_LN0B, ROW_NORM, ROW_RB, ROW_GB = 0, P, 2 * P, 4 * P, 4 * P + ROUNDS * EXPERTS
ROW_N = ROW_GB + ROUNDS * EXPERTS
WROWS = 2 * EXPERTS + SHARED

SIGNALS = [
    "x_loaded", "ctx_loaded", "bias_loaded", "stored",
    "var", "rstd", "xn", "xT", "h", "mixed", "r_ready", "k_ready", "v_ready", "sr", "kp", "args",
    "decays", "den", "inv", "act_own", "rwkv", "wo", "mixed2", "kf", "relu", "squared", "cr", "sig", "cv", "x_new",
    "qT", "kT", "vT", "k_kept", "high", "low", "v_kept", "windows", "dup", "dup_out", "dup_out2", "bias_split", "s_ready", "s_max",
    "mT", "mT_out", "st_ready", "probs", "pv", "heads_out", "logs", "inverse", "divided", "attn",
    "gate", "gate_max", "gate_exp", "w_split", "wT", "wT_out", "up", "h_out", "g_ready", "silu", "wb", "t_out",
    "z_part", "z_done",
    "next_var", "next_rstd",
]


def network(nc, xs, ctxT, biasT, bias_rows, wl, wx, we, wrout, vec, rows, bdown, const, dup, out):
    PAIRS = out.shape[0] // (ROWS * STREAMS)
    with ExitStack() as ctx:
        def sb(name, shape, dt=F32):
            return ctx.enter_context(nc.sbuf_tensor(name, shape, dt))

        def per_stream(name, shape, dt=F32):
            return [sb(f"{name}{s}", shape, dt) for s in range(STREAMS)]

        W = sb("W", [P, LAYERS * LAYER_W, P])
        WX = sb("WX", [P, 5, P])
        WE = sb("WE", [P, UNITS * 3, P])
        WROUT = sb("WROUT", [P, ROUNDS * EXPERTS])
        VECS = sb("VECS", [P, VEC_N])
        ROWB = sb("ROWB", [P, ROW_N])
        BDOWN = sb("BDOWN", [WROWS, P])
        CONST = sb("CONST", [P, P + 64])
        IDENT = CONST[:, 0:P]
        LOWER = CONST[:, P:P + EXPERTS * EXPERTS]
        PART = CONST[:, P + 36:P + 37]
        NEGEYE = CONST[:, P + 48:P + 48 + GROUPS]
        DUP = sb("DUP", [P, 4 * GROUPS, P], F32R)
        ONES2 = sb("ONES2", [P, P], F32R)
        WSEL = sb("WSEL", [WROWS, EXPERTS], F32R)
        NEGW = sb("NEGW", [P, LAYERS])
        ZTOP = sb("ZTOP", [P, LAYERS])
        WPAD = sb("WPAD", [P, LAYERS, ROWS * PAD])
        HALF = sb("HALF", [P, ROWS])

        x0 = per_stream("x0", [P, ROWS, P])
        x = per_stream("x", [P, ROWS, P])
        next_stats = per_stream("next_stats", [P, ROWS, 6])
        next_mvar = per_stream("next_mvar", [P, ROWS, 2])
        next_veps = per_stream("next_veps", [P, ROWS])
        next_rstd = per_stream("next_rstd", [P, ROWS])
        xn = per_stream("xn", [P, ROWS, P])
        hp = per_stream("hp", [P, ROWS, PAD])
        dh = per_stream("dh", [P, ROWS, P])
        mr = per_stream("mr", [P, N])
        mk = per_stream("mk", [P, N])
        mv = per_stream("mv", [P, N])
        sr = per_stream("sr", [P, N])
        kp = per_stream("kp", [P, ROWS, PAD])
        pp = per_stream("pp", [P, ROWS, PAD])
        aa = per_stream("aa", [P, ROWS, PAD])
        cc = per_stream("cc", [P, ROWS, PAD])
        cv = per_stream("cv", [P, ROWS, PAD])
        sa = per_stream("sa", [P, ROWS, PAD])
        sbb = per_stream("sbb", [P, ROWS, PAD])
        num = per_stream("num", [P, ROWS, P])
        kf = per_stream("kf", [P, FF, N])
        stats = per_stream("stats", [P, ROWS, 6])
        mvar = per_stream("mvar", [P, ROWS, 2])
        veps = per_stream("veps", [P, ROWS])
        rstd = per_stream("rstd", [P, ROWS])
        msq = per_stream("msq", [P, ROWS])

        ctxs = per_stream("ctxs", [P, N])
        hi = per_stream("hi", [P, N], F32R)
        lo = per_stream("lo", [P, N], F32R)
        qs = per_stream("qs", [P, GROUPS, N], F32R)
        ks = per_stream("ks", [P, GROUPS, N], F32R)
        vz = per_stream("vz", [P, GROUPS * DIAG])
        kbias = per_stream("kbias", [P, ROWS])
        bsp = per_stream("bsp", [P, N], F32R)
        smax = per_stream("smax", [P, 4, 32])

        gt = per_stream("gt", [P, ROWS, EXPERTS])
        bi = per_stream("bi", [P, ROWS, EXPERTS])
        cmp1 = per_stream("cmp1", [P, ROWS, EXPERTS * EXPERTS])
        cmp2 = per_stream("cmp2", [P, ROWS, EXPERTS * EXPERTS])
        rank = per_stream("rank", [P, ROWS, EXPERTS])
        gmax = per_stream("gmax", [P, ROWS])
        wts = per_stream("wts", [P, ROWS, WROWS])
        whi = per_stream("whi", [P, ROWS, EXPERTS], F32R)

        ps = [ctx.enter_context(nc.psum_tensor(f"ps{s}", [P, 4, N], F32)) for s in range(STREAMS)]

        def inner(t):
            return t[:, :, 1:PAD]

        def before(t):
            return t[:, :, 0:P]

        def windows(s, at):
            v = vz[s][:, :].rearrange("p (t r) -> p t r", r=DIAG)[:, :, 0:4 * 64]
            return v.rearrange("p t (g c) -> p t g c", c=64)[:, :, :, at:at + HEAD]

        def flat(t):
            return t[:, :, :].rearrange("p b t -> p (b t)")

        ee = den = dh
        zz = [inner(t) for t in pp]
        bhi = lo
        wT = [t[0:WROWS, :] for t in hi]
        xa = xn
        xT = mr
        probs = kf
        x1 = [t[:, 2, :].rearrange("p (b t) -> p b t", b=ROWS) for t in kf]
        vals = dh
        brow = [t[:, FF - 1, :] for t in kf]
        mT = [t[:, :].rearrange("p (g t) -> p g t", t=P) for t in hi]
        heads = [[mk[s][:, :], mv[s][:, :]] for s in range(STREAMS)]
        inv = [[sr[s][:, :], num[s][:, :, :].rearrange("p b t -> p (b t)")] for s in range(STREAMS)]
        h_e = [[mk[s][:, :], dh[s][:, :, :].rearrange("p b t -> p (b t)")] for s in range(STREAMS)]
        silu_e = [[mv[s][:, :], num[s][:, :, :].rearrange("p b t -> p (b t)")] for s in range(STREAMS)]
        t_e = [[sr[s][:, :], kf[s][:, 0, :]] for s in range(STREAMS)]

        setup = {n: ctx.enter_context(nc.semaphore("set_" + n)) for n in
                 ("loads", "dup_loads", "pads", "consts", "own", "half", "wx", "we")}
        w_loaded = [ctx.enter_context(nc.semaphore(f"w_loaded{l}")) for l in range(LAYERS)]
        sig = {n: [ctx.enter_context(nc.semaphore(f"{n}{s}")) for s in range(STREAMS)] for n in SIGNALS}
        dve_own = [ctx.enter_context(nc.semaphore(f"dve_own{s}")) for s in range(STREAMS)]
        used = [q for pair in sig.values() for q in pair] + dve_own

        def slots():
            for k in range(2 * LAYERS + 1):
                time_mix = (k % 2, k // 2) if k < 2 * LAYERS else None
                channel_mix = ((k - 1) % 2, (k - 1) // 2) if k else None
                yield time_mix, channel_mix

        def load_x(sp, s, first):
            sp.dma_start(x0[s][:, :, :], xs[bass.ds(first, ROWS), :, :].rearrange("b t c -> t b c")).then_inc(
                sig["x_loaded"][s], 16)

        steps = [0, 0]

        def done(s, ins):
            ins.then_inc(dve_own[s], 1)
            steps[s] += 1
            return steps[s]

        def ahead_stats(dve, s, src):
            for b in range(ROWS):
                n = done(s, nc.vector.bn_stats(next_stats[s][:, b, :], src[s][:, b, :]))
            dve.wait_ge(dve_own[s], n)
            for b in range(ROWS):
                n = done(s, nc.vector.bn_aggr(next_mvar[s][:, b, :], next_stats[s][:, b, :]))
            dve.wait_ge(dve_own[s], n)
            nc.vector.tensor_scalar(next_veps[s][:, :], next_mvar[s][:, :, 1], EPS, None, ALU.add).then_inc(
                sig["next_var"][s], 1)

        def ahead_norm(dve, s):
            dve.wait_ge(sig["next_rstd"][s], 1)
            for b in range(ROWS):
                n = done(s, nc.vector.tensor_scalar(x1[s][:, b, :], x0[s][:, b, :], next_mvar[s][:, b, 0:1],
                                                    next_rstd[s][:, b:b + 1], ALU.subtract, ALU.mult))
            dve.wait_ge(dve_own[s], n)
            row = ROWB[:, ROW_LN0W:ROW_LN0W + P].unsqueeze(1).broadcast_to([P, ROWS, P])
            n = done(s, nc.vector.tensor_tensor(x1[s], x1[s], row, ALU.mult))
            dve.wait_ge(dve_own[s], n)
            row = ROWB[:, ROW_LN0B:ROW_LN0B + P].unsqueeze(1).broadcast_to([P, ROWS, P])
            n = done(s, nc.vector.tensor_tensor(x1[s], x1[s], row, ALU.add))
            dve.wait_ge(dve_own[s], n)

        def ahead_root(pool, s, nth):
            pool.wait_ge(sig["next_var"][s], nth)
            nc.gpsimd.tensor_tensor(next_rstd[s][:, :], next_veps[s][:, :], HALF[:, :], ALU.pow).then_inc(
                sig["next_rstd"][s], 1)

        with nc.Block() as block:
            @block.sync
            def _(sp):
                for s in range(STREAMS):
                    load_x(sp, s, s * ROWS)
                sp.dma_start(VECS[:, :], vec).then_inc(setup["loads"], 16)
                sp.dma_start(ROWB[:, :], rows).then_inc(setup["loads"], 16)
                sp.dma_start(CONST[:, :], const).then_inc(setup["loads"], 16)
                for half in range(2):
                    sp.dma_start(kf[half][:, 0:2, :].rearrange("p a b -> p (a b)"), dup[:, half, :]).then_inc(
                        setup["dup_loads"], 16)
                sp.dma_start(BDOWN[:, :], bdown).then_inc(setup["dup_loads"], 16)
                sp.dma_start(WROUT[:, :], wrout).then_inc(setup["dup_loads"], 16)

            @block.scalar
            def _(act):
                for l in range(LAYERS):
                    if l == 1:
                        act.wait_ge(setup["loads"], 16 * 3)
                    act.dma_start(W[:, LAYER_W * l:LAYER_W * (l + 1), :], wl[:, LAYER_W * l:LAYER_W * (l + 1), :]
                                  ).then_inc(w_loaded[l], 16)
                act.dma_start(WX[:, :, :], wx).then_inc(setup["wx"], 16)
                act.dma_start(WE[:, :, :], we).then_inc(setup["we"], 16)
                nc.scalar.activation(NEGW[:, :], VECS[:, VEC["decay"]:VEC["decay"] + LAYERS], ACT.Exp).then_inc(
                    setup["own"], 1)

            @block.vector
            def _(dve):
                nc.vector.memset(HALF[:, :], -0.5).then_inc(setup["half"], 1)
                for s in range(STREAMS):
                    dve.wait_ge(sig["x_loaded"][s], 16)
                    ahead_stats(dve, s, x0)
                dve.wait_ge(setup["loads"], 16 * 3)
                for s in range(STREAMS):
                    ahead_norm(dve, s)
                    ahead_stats(dve, s, x1)
                nc.vector.tensor_copy(ONES2[:, :], CONST[:, P + 38:P + 39].broadcast_to([P, P]))
                nc.vector.tensor_copy(WSEL[:, :], CONST[0:WROWS, P + 40:P + 40 + EXPERTS])
                nc.vector.tensor_scalar(ZTOP[:, :], VECS[:, VEC["first"]:VEC["first"] + LAYERS], -1.0, TOP,
                                        ALU.mult, ALU.add)
                for s in range(STREAMS):
                    nc.vector.memset(wts[s][:, :, 2 * EXPERTS:WROWS], 1.0)
                dve.wait_ge(setup["own"], 1)
                dve.wait_ge(setup["pads"], 1)
                for l in range(LAYERS):
                    nc.vector.tensor_scalar(WPAD[:, l, :], WPAD[:, l, :], NEGW[:, l:l + 1], None,
                                            ALU.subtract).then_inc(setup["consts"], 1)
                dve.wait_ge(setup["consts"], LAYERS)
                wp = WPAD[:, :, :].rearrange("p l (b t) -> p (l b) t", t=PAD)
                nc.vector.memset(wp[:, :, 0:1], FAR)
                dve.wait_ge(setup["dup_loads"], 16 * 4)
                for half in range(2):
                    nc.vector.tensor_copy(
                        DUP[:, 2 * GROUPS * half:2 * GROUPS * (half + 1), :].rearrange("p a b -> p (a b)"),
                        kf[half][:, 0:2, :].rearrange("p a b -> p (a b)"))

            @block.gpsimd
            def _(pool):
                nc.gpsimd.memset(WPAD[:, :, :], 0.0).then_inc(setup["pads"], 1)
                pool.wait_ge(setup["half"], 1)
                for s in range(STREAMS):
                    ahead_root(pool, s, 1)
                for s in range(STREAMS):
                    nc.gpsimd.memset(hp[s][:, :, 0:1], 0.0)
                    nc.gpsimd.memset(kp[s][:, :, 0:1], FAR)
                    nc.gpsimd.memset(smax[s][:, :, :], 0.0)
                    nc.gpsimd.memset(vz[s][:, :], 0.0).then_inc(setup["pads"], 1)
                    pool.wait_ge(setup["pads"], s + 2)
                    nc.gpsimd.memset(windows(s, 32), 1.0)
                    for t in (aa, cc, cv):
                        nc.gpsimd.memset(t[s][:, :, 0:1], 0.0)
                for s in range(STREAMS):
                    ahead_root(pool, s, 2)
        nc.all_engine_barrier(sems_to_clear=range(used[0].num, used[-1].num + 1))

        with nc.Fori(0, PAIRS) as pair:
            with nc.Block() as block:
                both = range(STREAMS)

                @block.sync
                def _(sp):
                    for s in both:
                        first = pair * (STREAMS * ROWS) + s * ROWS
                        sp.dma_start(ctxs[s][:, :], ctxT[:, bass.ds(first * P, N)]).then_inc(
                            sig["ctx_loaded"][s], 16)
                        sp.dma_start(kbias[s][:, :], biasT[:, bass.ds(first, ROWS)]).then_inc(
                            sig["bias_loaded"][s], 16)
                    for s in both:
                        first = pair * (STREAMS * ROWS) + s * ROWS
                        sp.wait_ge(sig["cv"][s], LAYERS)
                        sp.dma_start(brow[s][:, :], bias_rows[:, bass.ds(first * P, N)]).then_inc(
                            sig["bias_loaded"][s], 16)
                    for s in both:
                        sp.wait_ge(sig["var"][s], 2 * LAYERS)
                        load_x(sp, s, pair * (STREAMS * ROWS) + (STREAMS + s) * ROWS)
                    for s in both:
                        first = pair * (STREAMS * ROWS) + s * ROWS
                        sp.wait_ge(sig["xn"][s], 2 * LAYERS + 4)
                        sp.dma_start(out[bass.ds(first, ROWS), :, :].rearrange("b t c -> t b c"), xn[s][:, :, :]
                                     ).then_inc(sig["stored"][s], 16)
                    for s in both:
                        sp.wait_ge(sig["stored"][s], 16)

                @block.gpsimd
                def _(pool):
                    norms = 2 * LAYERS + 1 + ROUNDS + 1
                    order = []
                    for time_mix, channel_mix in slots():
                        order += [part[0] for part in (time_mix, channel_mix) if part]
                    seen = [0, 0]
                    def root(s):
                        seen[s] += 1
                        pool.wait_ge(sig["var"][s], seen[s])
                        nc.gpsimd.tensor_tensor(rstd[s][:, :], veps[s][:, :], HALF[:, :], ALU.pow).then_inc(
                            sig["rstd"][s], 1)

                    for s in order:
                        root(s)
                    for s in both:
                        for tile in inv[s]:
                            nc.gpsimd.memset(tile, 0.0)
                    for b in range(ROWS):
                        for s in both:
                            pool.wait_ge(sig["v_kept"][s], 1)
                            if b:
                                pool.wait_ge(sig["pv"][s], b)
                            nc.gpsimd.tensor_copy(windows(s, 0), vals[s][:, b, :].rearrange(
                                "p (t g d) -> p t g d", g=4, d=HEAD)).then_inc(
                                sig["windows"][s], 1)
                    for n in range(norms - seen[0]):
                        for s in both:
                            root(s)
                        if n < 2:
                            for s in both:
                                ahead_root(pool, s, n + 1)

                @block.tensor
                def _(pe):
                    def transposes(s, src, bank):
                        for b in range(ROWS):
                            last = nc.tensor.transpose(ps[s][:, bank, b * P:(b + 1) * P], src[s][:, b, :], IDENT)
                        return last

                    def token_major(s, src, w, bank, first=True, stop=True):
                        for b in range(ROWS):
                            last = nc.tensor.matmul(ps[s][:, bank, b * P:(b + 1) * P], src[:, b * P:(b + 1) * P], w,
                                                    start=first and b == 0, stop=stop, skip_group_check=True)
                        return last

                    def product(s, w, src, bank, start=True, stop=True):
                        return nc.tensor.matmul(ps[s][:, bank, :], w, src, start=start, stop=stop)

                    def features(c, m, f):
                        product(c, W[:, LAYER_W * m + WCK + f, :], mk[c][:, :], f).then_inc(sig["kf"][c], 1)

                    def features_out(c, m, f):
                        pe.wait_ge(sig["squared"][c], FF * m + f + 1)
                        return token_major(c, kf[c][:, f, :], W[:, LAYER_W * m + WCV + f, :], 1, f == 0, f == FF - 1)

                    for time_mix, channel_mix in slots():
                        if time_mix:
                            s, l = time_mix
                            w = LAYER_W * l
                            pe.wait_ge(sig["xn"][s], 2 * l + 1)
                            transposes(s, xn, 0).then_inc(sig["xT"][s], 1)
                        if channel_mix:
                            c, m = channel_mix
                            v = LAYER_W * m
                            pe.wait_ge(sig["xn"][c], 2 * m + 2)
                            transposes(c, xn, 0).then_inc(sig["xT"][c], 1)
                        if time_mix:
                            pe.wait_ge(w_loaded[l], 16)
                            pe.wait_ge(sig["mixed"][s], 3 * l + 1)
                            product(s, W[:, w + WK, :], mk[s][:, :], 1).then_inc(sig["k_ready"][s], 1)
                            pe.wait_ge(sig["mixed"][s], 3 * l + 2)
                            product(s, W[:, w + WR, :], mr[s][:, :], 3).then_inc(sig["r_ready"][s], 1)
                            pe.wait_ge(sig["mixed"][s], 3 * l + 3)
                            product(s, W[:, w + WV, :], mv[s][:, :], 2).then_inc(sig["v_ready"][s], 1)
                        if channel_mix:
                            pe.wait_ge(sig["mixed2"][c], 2 * m + 1)
                            features(c, m, 0)
                        if channel_mix:
                            features(c, m, 1)
                        if channel_mix:
                            features(c, m, 2)
                            features(c, m, 3)
                            pe.wait_ge(sig["mixed2"][c], 2 * m + 2)
                            pe.wait_ge(sig["relu"][c], FF * m + 1)
                            token_major(c, mr[c], W[:, v + WCR, :], 0).then_inc(sig["cr"][c], 1)
                            features_out(c, m, 0)
                            features_out(c, m, 1)
                        if time_mix:
                            pe.wait_ge(sig["rwkv"][s], l + 1)
                            token_major(s, num[s][:, :, :].rearrange("p b t -> p (b t)"), W[:, w + WO, :], 0).then_inc(
                                sig["wo"][s], 1)
                        if channel_mix:
                            features_out(c, m, 2)
                            features_out(c, m, 3).then_inc(sig["cv"][c], 1)

                    def scores(s, rows_of, cols_of, toks):
                        for t in range(GROUPS):
                            for g in range(4):
                                part = slice(32 * g, 32 * g + 32)
                                last = nc.tensor.matmul(ps[s][:, g, t * P:(t + 1) * P], rows_of[s][part, t, toks],
                                                        cols_of[s][part, t, toks], start=False, stop=t == GROUPS - 1,
                                                        skip_group_check=True)
                        return last

                    pe.wait_ge(setup["wx"], 16)
                    for s in both:
                        pe.wait_ge(sig["relu"][s], FF * LAYERS)
                        pe.wait_ge(sig["ctx_loaded"][s], 16)
                        product(s, WX[:, 1, :], ctxs[s][:, :], 2).then_inc(sig["kT"][s], 1)
                        token_major(s, ctxs[s], WX[:, 2, :], 3).then_inc(sig["vT"][s], 1)
                    for s in both:
                        pe.wait_ge(sig["xn"][s], 2 * LAYERS + 1)
                        transposes(s, xn, 0).then_inc(sig["xT"][s], 1)
                    for s in both:
                        pe.wait_ge(sig["h"][s], 2 * LAYERS + 1)
                        product(s, WX[:, 0, :], xT[s][:, :], 1).then_inc(sig["qT"][s], 1)
                    for which in range(2):
                        for s in both:
                            pe.wait_ge(sig["high"][s], which + 1)
                            pe.wait_ge(sig["low"][s], which + 1)
                            if which == 0:
                                pe.wait_ge(sig["v_kept"][s], 1)
                                pe.wait_ge(sig["k_kept"][s], 1)
                            for t in range(GROUPS):
                                if which == 1:
                                    pe.wait_ge(sig["dup_out2" if t % 2 else "dup_out"][s], t // 2 + 1)
                                at = 2 * GROUPS * which + t
                                nc.tensor.matmul(ps[s][:, t, :], DUP[:, at, :], hi[s][:, :], start=True, stop=False)
                                nc.tensor.matmul(ps[s][:, t, :], DUP[:, at + GROUPS, :], lo[s][:, :], start=False,
                                                 stop=True).then_inc(sig["dup"][s], 1)
                    def scores_by_query(s, b):
                        toks = slice(b * P, (b + 1) * P)
                        if b == 0:
                            pe.wait_ge(sig["dup_out"][s], GROUPS)
                            pe.wait_ge(sig["dup_out2"][s], GROUPS)
                            pe.wait_ge(sig["bias_split"][s], 1)
                        else:
                            pe.wait_ge(sig["heads_out"][s], b)
                        for g in range(4):
                            parts = slice(32 * g, 32 * g + 2)
                            bias = bsp[s][parts, toks].unsqueeze(1).broadcast_to([2, 4, P])
                            nc.tensor.matmul(ps[s][:, g, :].rearrange("p (t k) -> p t k", t=4), ONES2[parts, :], bias,
                                             start=True, stop=False, skip_group_check=True)
                        scores(s, qs, ks, toks).then_inc(sig["s_ready"][s], 1)

                    def turn_maxima(s, b):
                        pe.wait_ge(sig["s_max"][s], b + 1)
                        nc.tensor.transpose(ps[s][:, 0, 0:P], smax[s][:, :, :].rearrange("p g t -> p (g t)"),
                                            IDENT).then_inc(sig["mT"][s], 1)

                    def scores_by_key(s, b):
                        pe.wait_ge(sig["mT_out"][s], b + 1)
                        for g in range(4):
                            parts = slice(32 * g, 32 * g + GROUPS)
                            nc.tensor.matmul(ps[s][:, g, :], ONES2[parts, :],
                                             mT[s][parts, :, :].rearrange("p t q -> p (t q)"),
                                             start=True, stop=False, skip_group_check=True)
                        scores(s, ks, qs, slice(b * P, (b + 1) * P)).then_inc(sig["st_ready"][s], 1)

                    def weighted(s, b):
                        pe.wait_ge(sig["probs"][s], b + 1)
                        pe.wait_ge(sig["windows"][s], b + 1)
                        for g in range(4):
                            for t in range(GROUPS):
                                at = 64 * (4 * t + g)
                                half = 64 * (g % 2)
                                last = nc.tensor.matmul(
                                    ps[s][half:half + 64, 0, (g // 2) * P:(g // 2 + 1) * P],
                                    vz[s][:, at:at + 64], probs[s][:, g, t * P:(t + 1) * P],
                                    start=g < 2 and t == 0, stop=t == GROUPS - 1, skip_group_check=True)
                        last.then_inc(sig["pv"][s], 1)

                    for b in range(ROWS):
                        for s in both:
                            scores_by_query(s, b)
                        for s in both:
                            turn_maxima(s, b)
                            scores_by_key(s, b)
                        for s in both:
                            weighted(s, b)
                    for s in both:
                        pe.wait_ge(sig["divided"][s], 1)
                        token_major(s, heads[s][0], WX[:, 3, :], 1, True, False)
                        pe.wait_ge(sig["divided"][s], 2)
                        token_major(s, heads[s][1], WX[:, 4, :], 1, False, True).then_inc(sig["attn"][s], 1)

                    pe.wait_ge(setup["we"], 16)
                    for j in range(ROUNDS):
                        for s in both:
                            if j == 0:
                                pe.wait_ge(sig["xn"][s], 2 * LAYERS + 2)
                            else:
                                pe.wait_ge(sig["x_new"][s], j)
                            transposes(s, x if j else xn, 0).then_inc(sig["xT"][s], 1)
                        def up(u):
                            for s in both:
                                if u:
                                    pe.wait_ge(sig["h_out"][s], UNITS * j + u)
                                else:
                                    pe.wait_ge(sig["h"][s], 2 * LAYERS + 2 + j)
                                product(s, WE[:, u, :], xT[s][:, :], 0).then_inc(sig["up"][s], 1)

                        def gate(u):
                            n = UNITS * j + u
                            for s in both:
                                pe.wait_ge(sig["h_out"][s], n + 1)
                                if n:
                                    pe.wait_ge(sig["silu"][s], n)
                                product(s, WE[:, UNITS + u, :], h_e[s][u % 2], 1).then_inc(sig["g_ready"][s], 1)

                        up(0)
                        for s in both:
                            for b in range(ROWS):
                                last = nc.tensor.matmul(ps[s][:, 2, b * EXPERTS:(b + 1) * EXPERTS],
                                                        xT[s][:, b * P:(b + 1) * P],
                                                        WROUT[:, j * EXPERTS:(j + 1) * EXPERTS],
                                                        start=b == 0, stop=True, skip_group_check=True)
                            last.then_inc(sig["gate"][s], 1)
                        gate(0)
                        up(1)
                        for u in range(UNITS):
                            n = UNITS * j + u
                            if u == SHARED:
                                for s in both:
                                    pe.wait_ge(sig["w_split"][s], j + 1)
                                    for b in range(ROWS):
                                        last = nc.tensor.transpose(ps[s][0:WROWS, 2, b * P:(b + 1) * P], wts[s][:, b, :],
                                                                   IDENT)
                                    last.then_inc(sig["wT"][s], 1)
                            if u >= SHARED:
                                for s in both:
                                    if u == SHARED:
                                        pe.wait_ge(sig["wT_out"][s], j + 1)
                                    else:
                                        pe.wait_ge(sig["t_out"][s], n)
                                    product(s, WSEL[:, u - SHARED:u - SHARED + 1].broadcast_to([WROWS, P]), wT[s][:, :],
                                            2).then_inc(sig["wb"][s], 1)
                            if u < UNITS - 1:
                                gate(u + 1)
                            for s in both:
                                pe.wait_ge(sig["t_out"][s], n + 1)
                                token_major(s, t_e[s][u % 2], WE[:, 2 * UNITS + u, :], 3, u == 0, False).then_inc(
                                    sig["z_part"][s], 1)
                            if u < UNITS - 2:
                                up(u + 2)
                        for s in both:
                            for b in range(ROWS):
                                last = nc.tensor.matmul(ps[s][:, 3, b * P:(b + 1) * P],
                                                        wT[s][:, b * P:(b + 1) * P].bitcast(F32), BDOWN[:, :],
                                                        start=False, stop=True, skip_group_check=True)
                            last.then_inc(sig["z_done"][s], 1)

                @block.scalar
                def _(act):
                    def vecs(name, l):
                        return VECS[:, VEC[name] + l:VEC[name] + l + 1]

                    def normed_h(s, l, half):
                        act.wait_ge(sig["xT"][s], 2 * l + half)
                        nc.scalar.activation(inner(hp[s]), ps[s][:, 0, :].rearrange("p (b t) -> p b t", t=P),
                                             ACT.Identity, scale=vecs(f"ln{half}_w", l),
                                             bias=vecs(f"ln{half}_b", l)).then_inc(sig["h"][s], 1)

                    def relu(c, m, f):
                        act.wait_ge(sig["kf"][c], FF * m + f + 1)
                        nc.scalar.activation(kf[c][:, f, :], ps[c][:, f, :], ACT.Relu).then_inc(sig["relu"][c], 1)

                    def square(c, m, f):
                        act.wait_ge(sig["relu"][c], FF * m + f + 1)
                        nc.scalar.activation(kf[c][:, f, :], kf[c][:, f, :], ACT.Square).then_inc(
                            sig["squared"][c], 1)

                    for time_mix, channel_mix in slots():
                        if time_mix:
                            s, l = time_mix
                            normed_h(s, l, 1)
                        if channel_mix:
                            c, m = channel_mix
                            normed_h(c, m, 2)
                        if time_mix:
                            act.wait_ge(sig["k_ready"][s], l + 1)
                            nc.scalar.activation(inner(kp[s]), ps[s][:, 1, :].rearrange("p (b t) -> p b t", t=P),
                                                 ACT.Identity).then_inc(sig["kp"][s], 1)
                            act.wait_ge(sig["r_ready"][s], l + 1)
                            nc.scalar.activation(sr[s][:, :], ps[s][:, 3, :], ACT.Sigmoid).then_inc(sig["sr"][s], 1)
                        elif channel_mix:
                            relu(c, m, 0)
                            relu(c, m, 1)
                        if time_mix:
                            nc.scalar.preload_act_table_set("natural_log_exp_and_others")
                            act.wait_ge(sig["args"][s], 3 * l + 1)
                            nc.scalar.activation(inner(cc[s]), inner(cc[s]), ACT.Exp).then_inc(sig["decays"][s], 1)
                            act.wait_ge(sig["args"][s], 3 * l + 2)
                            nc.scalar.activation(inner(aa[s]), inner(aa[s]), ACT.Exp, scale=-1.0).then_inc(
                                sig["decays"][s], 1)
                            act.wait_ge(sig["args"][s], 3 * l + 3)
                            nc.scalar.activation(zz[s], zz[s], ACT.Exp, bias=vecs("first", l)).then_inc(
                                sig["decays"][s], 1)
                            if channel_mix:
                                relu(c, m, 0)
                                relu(c, m, 1)
                        if channel_mix:
                            relu(c, m, 2)
                            relu(c, m, 3)
                            square(c, m, 0)
                            square(c, m, 1)
                        if time_mix:
                            act.wait_ge(sig["den"][s], l + 1)
                            nc.scalar.activation(den[s][:, :, :], den[s][:, :, :], ACT.Ln).then_inc(
                                sig["act_own"][s], 1)
                            act.wait_ge(sig["act_own"][s], l + 1)
                            nc.scalar.activation(den[s][:, :, :], den[s][:, :, :], ACT.Exp, scale=-1.0).then_inc(
                                sig["inv"][s], 1)
                        if channel_mix:
                            square(c, m, 2)
                            square(c, m, 3)
                            act.wait_ge(sig["cr"][c], m + 1)
                            nc.scalar.activation(sr[c][:, :], ps[c][:, 0, :], ACT.Sigmoid).then_inc(sig["sig"][c], 1)

                    for s in both:
                        act.wait_ge(sig["xT"][s], 2 * LAYERS + 1)
                        nc.scalar.activation(xT[s][:, :], ps[s][:, 0, :], ACT.Identity).then_inc(sig["h"][s], 1)
                    for s in both:
                        act.wait_ge(sig["vT"][s], 1)
                        nc.scalar.activation(vals[s][:, :, :], ps[s][:, 3, :].rearrange("p (b c) -> p b c", b=ROWS),
                                             ACT.Identity).then_inc(sig["v_kept"][s], 1)
                    for which in range(2):
                        for s in both:
                            if which == 0:
                                act.wait_ge(sig["qT"][s], 1)
                            else:
                                act.wait_ge(sig["low"][s], 1)
                                act.wait_ge(sig["k_kept"][s], 1)
                                act.wait_ge(sig["dup"][s], GROUPS)
                            source = ps[s][:, 1, :] if which == 0 else mv[s][:, :]
                            nc.scalar.activation(hi[s][:, :], source, ACT.Identity).then_inc(sig["high"][s], 1)
                            if which == 0:
                                act.wait_ge(sig["kT"][s], 1)
                                nc.scalar.activation(mv[s][:, :], ps[s][:, 2, :], ACT.Identity).then_inc(
                                    sig["k_kept"][s], 1)
                        for s in both:
                            dst = ks if which else qs
                            for t in range(0, GROUPS, 2):
                                act.wait_ge(sig["dup"][s], GROUPS * which + t + 1)
                                nc.scalar.activation(dst[s][:, t, :], ps[s][:, t, :], ACT.Identity).then_inc(
                                    sig["dup_out"][s], 1)
                    nc.scalar.preload_act_table_set("natural_log_exp_and_others")
                    def exponentials(s, b):
                        act.wait_ge(sig["st_ready"][s], b + 1)
                        act.wait_ge(sig["bias_loaded"][s], 32)
                        if b:
                            act.wait_ge(sig["pv"][s], b)
                        nc.scalar.activation(probs[s][:, :, :].rearrange("p a b -> p (a b)"),
                                             ps[s][:, :, :].rearrange("p a b -> p (a b)"), ACT.Exp,
                                             bias=kbias[s][:, b:b + 1], scale=HEAD ** -0.5).then_inc(
                            sig["probs"][s], 1)

                    def heads_to_sbuf(s, b):
                        act.wait_ge(sig["pv"][s], b + 1)
                        for k in range(2):
                            last = nc.scalar.activation(heads[s][k][:, b * P:(b + 1) * P],
                                                        ps[s][:, 0, k * P:(k + 1) * P], ACT.Identity)
                        last.then_inc(sig["heads_out"][s], 1)

                    def logs(s, b):
                        act.wait_ge(sig["heads_out"][s], b + 1)
                        act.wait_ge(sig["windows"][s], 1)
                        for k in range(2):
                            for q in (0, 64):
                                last = nc.scalar.activation(inv[s][k][q:q + 32, b * P:(b + 1) * P],
                                                            heads[s][k][q + 32:q + 64, b * P:(b + 1) * P], ACT.Ln)
                        last.then_inc(sig["logs"][s], 1)

                    for b in range(ROWS):
                        for s in both:
                            exponentials(s, b)
                        for s in both:
                            heads_to_sbuf(s, b)
                        for s in both:
                            logs(s, b)
                    for s in both:
                        act.wait_ge(sig["logs"][s], ROWS)
                        for k in range(2):
                            nc.scalar.activation(inv[s][k], inv[s][k], ACT.Exp, scale=-1.0).then_inc(
                                sig["inverse"][s], 1)

                    for j in range(ROUNDS):
                        for s in both:
                            act.wait_ge(sig["xT"][s], 2 * LAYERS + 2 + j)
                            nc.scalar.activation(xT[s][:, :], ps[s][:, 0, :], ACT.Identity).then_inc(sig["h"][s], 1)
                        def up_out(u):
                            n = UNITS * j + u
                            at = VEC_SBUP + u if u < SHARED else VEC_BUP + u - SHARED
                            for s in both:
                                act.wait_ge(sig["up"][s], n + 1)
                                if n > 1:
                                    act.wait_ge(sig["t_out"][s], n - 1)
                                nc.scalar.activation(h_e[s][u % 2], ps[s][:, 0, :], ACT.Identity,
                                                     bias=VECS[:, at:at + 1]).then_inc(sig["h_out"][s], 1)

                        up_out(0)
                        for u in range(UNITS):
                            n = UNITS * j + u
                            at = VEC_SBG if u < SHARED else VEC_BG + u - SHARED
                            for s in both:
                                act.wait_ge(sig["g_ready"][s], n + 1)
                                nc.scalar.activation(silu_e[s][u % 2], ps[s][:, 1, :], ACT.Silu,
                                                     bias=VECS[:, at:at + 1]).then_inc(sig["silu"][s], 1)
                            if u < UNITS - 1:
                                up_out(u + 1)
                            if u == 0:
                                for s in both:
                                    act.wait_ge(sig["gate_max"][s], j + 1)
                                    nc.scalar.activation(gt[s][:, :, :], gt[s][:, :, :], ACT.Exp).then_inc(
                                        sig["gate_exp"][s], 1)
                            if u == SHARED:
                                for s in both:
                                    act.wait_ge(sig["wT"][s], j + 1)
                                    nc.scalar.activation(wT[s], ps[s][0:WROWS, 2, :], ACT.Identity).then_inc(
                                        sig["wT_out"][s], 1)

                @block.vector
                def _(dve):
                    norms = [0, 0]
                    halves = [0, 0]
                    steps[:] = [0, 0]

                    def need(s, n):
                        dve.wait_ge(dve_own[s], n)

                    def variances(s, src, eps, rms=False):
                        for b in range(ROWS):
                            n = done(s, nc.vector.bn_stats(stats[s][:, b, :], src[s][:, b, :]))
                        need(s, n)
                        for b in range(ROWS):
                            n = done(s, nc.vector.bn_aggr(mvar[s][:, b, :], stats[s][:, b, :]))
                        need(s, n)
                        if rms:
                            n = done(s, nc.vector.tensor_tensor(msq[s][:, :], mvar[s][:, :, 0], mvar[s][:, :, 0],
                                                                ALU.mult))
                            need(s, n)
                            nc.vector.scalar_tensor_tensor(veps[s][:, :], msq[s][:, :], eps, mvar[s][:, :, 1],
                                                           ALU.add, ALU.add).then_inc(sig["var"][s], 1)
                        else:
                            nc.vector.tensor_scalar(veps[s][:, :], mvar[s][:, :, 1], eps, None, ALU.add).then_inc(
                                sig["var"][s], 1)

                    def normed(s, dst, src):
                        norms[s] += 1
                        dve.wait_ge(sig["rstd"][s], norms[s])
                        for b in range(ROWS):
                            last = nc.vector.tensor_scalar(dst[s][:, b, :], src[s][:, b, :], mvar[s][:, b, 0:1],
                                                           rstd[s][:, b:b + 1], ALU.subtract, ALU.mult)
                        return last

                    def vecs(name, l):
                        return VECS[:, VEC[name] + l:VEC[name] + l + 1]

                    def back(s, l, n):
                        dve.wait_ge(sig["h"][s], 2 * l + n)
                        need(s, done(s, nc.vector.tensor_tensor(dh[s][:, :, :], inner(hp[s]), before(hp[s]),
                                                                ALU.subtract)))

                    def mix(s, l, dst, name):
                        return nc.vector.scalar_tensor_tensor(
                            dst[s][:, :].rearrange("p (b t) -> p b t", t=P), dh[s][:, :, :], vecs(name, l),
                            before(hp[s]), ALU.mult, ALU.add)

                    for time_mix, channel_mix in slots():
                        if time_mix:
                            s, l = time_mix
                            if l:
                                normed(s, xn, x).then_inc(sig["xn"][s], 1)
                            else:
                                for b in range(ROWS):
                                    last = nc.vector.tensor_scalar(
                                        xn[s][:, b, :], x1[s][:, b, :], next_mvar[s][:, b, 0:1],
                                        next_rstd[s][:, b:b + 1], ALU.subtract, ALU.mult)
                                last.then_inc(sig["xn"][s], 1)
                        if channel_mix:
                            c, m = channel_mix
                            normed(c, xn, x).then_inc(sig["xn"][c], 1)
                        if time_mix:
                            back(s, l, 1)
                            mix(s, l, mk, "tmk").then_inc(sig["mixed"][s], 1)
                            mix(s, l, mr, "tmr").then_inc(sig["mixed"][s], 1)
                        if channel_mix:
                            back(c, m, 2)
                            mix(c, m, mk, "cmk").then_inc(sig["mixed2"][c], 1)
                        if time_mix:
                            mix(s, l, mv, "tmv").then_inc(sig["mixed"][s], 1)
                        if channel_mix and not time_mix:
                            mix(c, m, mr, "cmr").then_inc(sig["mixed2"][c], 1)
                        if time_mix:
                            dve.wait_ge(sig["kp"][s], l + 1)
                            need(s, done(s, nc.vector.tensor_tensor_scan(flat(pp[s]), WPAD[:, l, :], flat(kp[s]), FAR,
                                                                         ALU.add, ALU.max)))
                            need(s, done(s, nc.vector.tensor_tensor(ee[s][:, :, :], inner(kp[s]), before(pp[s]),
                                                                    ALU.subtract)))
                            nc.vector.tensor_scalar(inner(cc[s]), ee[s][:, :, :], NEGW[:, l:l + 1], 0.0, ALU.add,
                                                    ALU.min).then_inc(sig["args"][s], 1)
                            nc.vector.tensor_scalar(inner(aa[s]), ee[s][:, :, :], NEGW[:, l:l + 1], 0.0, ALU.add,
                                                    ALU.max).then_inc(sig["args"][s], 1)
                            nc.vector.tensor_scalar(zz[s], ee[s][:, :, :], ZTOP[:, l:l + 1], None,
                                                    ALU.min).then_inc(sig["args"][s], 1)
                            if channel_mix:
                                mix(c, m, mr, "cmr").then_inc(sig["mixed2"][c], 1)
                            v = ps[s][:, 2, :].rearrange("p (b t) -> p b t", t=P)
                            dve.wait_ge(sig["v_ready"][s], l + 1)
                            dve.wait_ge(sig["decays"][s], 3 * l + 1)
                            n_cv = done(s, nc.vector.tensor_tensor(inner(cv[s]), inner(cc[s]), v, ALU.mult))
                            dve.wait_ge(sig["decays"][s], 3 * l + 2)
                            n_b = done(s, nc.vector.tensor_tensor_scan(flat(sbb[s]), flat(aa[s]), flat(cc[s]), 0.0,
                                                                       ALU.mult, ALU.add))
                            dve.wait_ge(sig["decays"][s], 3 * l + 3)
                            done(s, nc.vector.tensor_tensor(num[s][:, :, :], zz[s], v, ALU.mult))
                            need(s, n_b)
                            nc.vector.tensor_tensor(den[s][:, :, :], zz[s], before(sbb[s]), ALU.add).then_inc(
                                sig["den"][s], 1)
                            need(s, n_cv)
                            n_a = done(s, nc.vector.tensor_tensor_scan(flat(sa[s]), flat(aa[s]), flat(cv[s]), 0.0,
                                                                       ALU.mult, ALU.add))
                            need(s, n_a)
                            need(s, done(s, nc.vector.tensor_tensor(num[s][:, :, :], num[s][:, :, :], before(sa[s]),
                                                                    ALU.add)))
                            dve.wait_ge(sig["sr"][s], l + 1)
                            n_sr = done(s, nc.vector.tensor_tensor(
                                num[s][:, :, :], num[s][:, :, :], sr[s][:, :].rearrange("p (b t) -> p b t", t=P),
                                ALU.mult))
                            dve.wait_ge(sig["inv"][s], l + 1)
                            need(s, n_sr)
                            nc.vector.tensor_tensor(num[s][:, :, :], num[s][:, :, :], den[s][:, :, :],
                                                    ALU.mult).then_inc(sig["rwkv"][s], 1)
                        if time_mix:
                            dve.wait_ge(sig["wo"][s], l + 1)
                            need(s, done(s, nc.vector.tensor_tensor(
                                x[s][:, :, :], x[s][:, :, :] if l else x1[s], ps[s][:, 0, :].rearrange("p (b t) -> p b t", t=P),
                                ALU.add)))
                            variances(s, x, EPS)
                        if channel_mix:
                            dve.wait_ge(sig["sig"][c], m + 1)
                            dve.wait_ge(sig["cv"][c], m + 1)
                            need(c, done(c, nc.vector.tensor_tensor(sr[c][:, :], sr[c][:, :], ps[c][:, 1, :],
                                                                    ALU.mult)))
                            need(c, done(c, nc.vector.tensor_tensor(
                                x[c][:, :, :], x[c][:, :, :], sr[c][:, :].rearrange("p (b t) -> p b t", t=P), ALU.add)))
                            if m == LAYERS - 1:
                                need(c, done(c, nc.vector.tensor_tensor(x[c][:, :, :], x[c][:, :, :], x0[c][:, :, :],
                                                                        ALU.add)))
                            variances(c, x, EPS)

                    for s in both:
                        normed(s, xa, x).then_inc(sig["xn"][s], 1)
                    for s in both:
                        dve.wait_ge(sig["bias_loaded"][s], 32)
                        need(s, done(s, nc.vector.tensor_scalar(brow[s][:, :], brow[s][:, :], HEAD ** 0.5, None,
                                                                ALU.mult)))
                        need(s, done(s, nc.vector.tensor_copy(bhi[s][:, :], brow[s][:, :])))
                        need(s, done(s, nc.vector.tensor_scalar(bhi[s][:, :], bhi[s][:, :].bitcast(F32), PART, None,
                                                                ALU.mult)))
                        nc.vector.tensor_tensor(bsp[s][:, :], brow[s][:, :], bhi[s][:, :].bitcast(F32),
                                                ALU.subtract).then_inc(sig["bias_split"][s], 1)
                    for which in range(2):
                        for s in both:
                            dve.wait_ge(sig["high"][s], which + 1)
                            if which == 1:
                                dve.wait_ge(sig["dup"][s], GROUPS)
                            else:
                                dve.wait_ge(sig["bias_split"][s], 1)
                            source = ps[s][:, 1, :] if which == 0 else mv[s][:, :]
                            nc.vector.tensor_tensor(lo[s][:, :], source, hi[s][:, :].bitcast(F32),
                                                    ALU.subtract).then_inc(sig["low"][s], 1)
                        for s in both:
                            dst = ks if which else qs
                            for t in range(1, GROUPS, 2):
                                dve.wait_ge(sig["dup"][s], GROUPS * which + t + 1)
                                nc.vector.tensor_copy(dst[s][:, t, :], ps[s][:, t, :]).then_inc(
                                    sig["dup_out2"][s], 1)
                    def maxima(s, b):
                        dve.wait_ge(sig["s_ready"][s], b + 1)
                        nc.vector.tensor_reduce(smax[s][:, :, 0:GROUPS],
                                                ps[s][:, :, :].rearrange("p g (t k) -> p g t k", k=P),
                                                AX.X, ALU.max).then_inc(sig["s_max"][s], 1)

                    def maxima_to_blocks(s, b):
                        dve.wait_ge(sig["mT"][s], b + 1)
                        nc.vector.tensor_tensor(mT[s][:, :, :],
                                                ps[s][:, 0, 0:P].unsqueeze(1).broadcast_to([P, GROUPS, P]),
                                                NEGEYE.unsqueeze(2).broadcast_to([P, GROUPS, P]),
                                                ALU.mult).then_inc(sig["mT_out"][s], 1)

                    for b in range(ROWS):
                        for s in both:
                            maxima(s, b)
                            maxima_to_blocks(s, b)
                    for s in both:
                        for k in range(2):
                            dve.wait_ge(sig["inverse"][s], k + 1)
                            nc.vector.tensor_tensor(heads[s][k], heads[s][k], inv[s][k], ALU.mult).then_inc(
                                sig["divided"][s], 1)
                    for s in both:
                        dve.wait_ge(sig["attn"][s], 1)
                        need(s, done(s, nc.vector.tensor_tensor(
                            x[s][:, :, :], xa[s][:, :, :], ps[s][:, 1, :].rearrange("p (b t) -> p b t", t=P), ALU.add)))
                        variances(s, x, EPS)
                    for s in both:
                        normed(s, xa, x).then_inc(sig["xn"][s], 1)

                    for j in range(ROUNDS):
                        rb = ROWB[:, ROW_RB + j * EXPERTS:ROW_RB + (j + 1) * EXPERTS].unsqueeze(1).broadcast_to(
                            [P, ROWS, EXPERTS])
                        gb = ROWB[:, ROW_GB + j * EXPERTS:ROW_GB + (j + 1) * EXPERTS].unsqueeze(1).broadcast_to(
                            [P, ROWS, EXPERTS])
                        for s in both:
                            dve.wait_ge(sig["gate"][s], j + 1)
                            need(s, done(s, nc.vector.tensor_tensor(
                                gt[s][:, :, :], ps[s][:, 2, 0:ROWS * EXPERTS].rearrange("p (b e) -> p b e", e=EXPERTS),
                                rb, ALU.add)))
                            need(s, done(s, nc.vector.tensor_tensor(bi[s][:, :, :], gt[s][:, :, :], gb, ALU.add)))
                            for b in range(ROWS):
                                shape = [P, EXPERTS, EXPERTS]
                                other = bi[s][:, b, :].unsqueeze(1).broadcast_to(shape)
                                own = bi[s][:, b, :].unsqueeze(2).broadcast_to(shape)
                                c1 = cmp1[s][:, b, :].rearrange("p (e f) -> p e f", f=EXPERTS)
                                c2 = cmp2[s][:, b, :].rearrange("p (e f) -> p e f", f=EXPERTS)
                                done(s, nc.vector.tensor_tensor(c1, other, own, ALU.is_gt))
                                n = done(s, nc.vector.tensor_tensor(c2, other, own, ALU.is_equal))
                            need(s, n)
                            lower = LOWER.unsqueeze(1).broadcast_to([P, ROWS, EXPERTS * EXPERTS])
                            need(s, done(s, nc.vector.tensor_tensor(cmp2[s][:, :, :], cmp2[s][:, :, :], lower,
                                                                    ALU.mult)))
                            need(s, done(s, nc.vector.tensor_tensor(cmp1[s][:, :, :], cmp1[s][:, :, :],
                                                                    cmp2[s][:, :, :], ALU.add)))
                            need(s, done(s, nc.vector.tensor_reduce(
                                rank[s][:, :, :].rearrange("p b e -> p (b e)"),
                                cmp1[s][:, :, :].rearrange("p b (e f) -> p (b e) f", f=EXPERTS), AX.X, ALU.add)))
                            need(s, done(s, nc.vector.tensor_scalar(rank[s][:, :, :], rank[s][:, :, :], 1.5, -1e30,
                                                                    ALU.is_gt, ALU.mult)))
                            need(s, done(s, nc.vector.tensor_tensor(gt[s][:, :, :], gt[s][:, :, :], rank[s][:, :, :],
                                                                    ALU.add)))
                            need(s, done(s, nc.vector.tensor_reduce(gmax[s][:, :], gt[s][:, :, :], AX.X, ALU.max)))
                            nc.vector.tensor_tensor(gt[s][:, :, :], gt[s][:, :, :],
                                                    gmax[s][:, :].unsqueeze(2).broadcast_to([P, ROWS, EXPERTS]),
                                                    ALU.subtract).then_inc(sig["gate_max"][s], 1)
                        for u in range(UNITS):
                            n = UNITS * j + u
                            for s in both:
                                dve.wait_ge(sig["silu"][s], n + 1)
                                if n > 1:
                                    dve.wait_ge(sig["z_part"][s], n - 1)
                                mul = nc.vector.tensor_tensor(t_e[s][u % 2], silu_e[s][u % 2], h_e[s][u % 2], ALU.mult)
                                if u < SHARED:
                                    mul.then_inc(sig["t_out"][s], 1)
                                else:
                                    halves[s] = done(s, mul)
                            if u == 0:
                                for s in both:
                                    dve.wait_ge(sig["gate_exp"][s], j + 1)
                                    need(s, done(s, nc.vector.tensor_reduce(gmax[s][:, :], gt[s][:, :, :], AX.X, ALU.add)))
                                    need(s, done(s, nc.vector.reciprocal(gmax[s][:, :], gmax[s][:, :])))
                                    need(s, done(s, nc.vector.tensor_tensor(
                                        gt[s][:, :, :], gt[s][:, :, :],
                                        gmax[s][:, :].unsqueeze(2).broadcast_to([P, ROWS, EXPERTS]), ALU.mult)))
                                    need(s, done(s, nc.vector.tensor_copy(whi[s][:, :, :], gt[s][:, :, :])))
                                    n1 = done(s, nc.vector.tensor_copy(wts[s][:, :, 0:EXPERTS], whi[s][:, :, :].bitcast(F32)))
                                    need(s, n1)
                                    nc.vector.tensor_tensor(wts[s][:, :, EXPERTS:2 * EXPERTS], gt[s][:, :, :],
                                                            whi[s][:, :, :].bitcast(F32), ALU.subtract).then_inc(
                                        sig["w_split"][s], 1)
                            if u >= SHARED:
                                for s in both:
                                    need(s, halves[s])
                                    dve.wait_ge(sig["wb"][s], EXPERTS * j + u - SHARED + 1)
                                    nc.vector.tensor_tensor(t_e[s][u % 2], t_e[s][u % 2], ps[s][:, 2, :],
                                                            ALU.mult).then_inc(sig["t_out"][s], 1)
                            if u > SHARED:
                                step, s = divmod(u - SHARED - 1, STREAMS)
                                if (j, step) == (0, 0):
                                    dve.wait_ge(sig["x_loaded"][s], 16)
                                    ahead_stats(dve, s, x0)
                                elif (j, step) == (0, 1):
                                    ahead_norm(dve, s)
                                elif (j, step) == (1, 0):
                                    ahead_stats(dve, s, x1)
                        for s in both:
                            src = x if j else xa
                            dve.wait_ge(sig["z_done"][s], j + 1)
                            need(s, done(s, nc.vector.tensor_tensor(
                                x[s][:, :, :], src[s][:, :, :], ps[s][:, 3, :].rearrange("p (b t) -> p b t", t=P),
                                ALU.add)))
                            variances(s, x, RMS_EPS, rms=True)
                        for s in both:
                            norms[s] += 1
                            dve.wait_ge(sig["rstd"][s], norms[s])
                            for b in range(ROWS):
                                last = nc.vector.scalar_tensor_tensor(
                                    x[s][:, b, :], x[s][:, b, :], rstd[s][:, b:b + 1],
                                    ROWB[:, ROW_NORM + j * P:ROW_NORM + (j + 1) * P], ALU.mult, ALU.mult)
                            last.then_inc(sig["x_new"][s], 1)
                    for s in both:
                        dve.wait_ge(sig["x_new"][s], ROUNDS)
                        need(s, done(s, nc.vector.tensor_tensor(x[s][:, :, :], x[s][:, :, :], xa[s][:, :, :],
                                                                ALU.add)))
                        variances(s, x, EPS)
                    for s in both:
                        normed(s, xn, x).then_inc(sig["xn"][s], 2)
            nc.all_engine_barrier(sems_to_clear=range(used[0].num, used[-1].num + 1))


def kernel(**inputs):
    import numpy as np
    import concourse.bacc as bacc
    from concourse import mybir as mb
    from concourse.bass_utils import run_bass_kernel_spmd

    a = {k: np.asarray(v) for k, v in inputs.items()}
    r = {k[8:]: v for k, v in a.items() if k.startswith("L0_attn_")}
    t = {k[9:]: v for k, v in a.items() if k.startswith("L0_xattn_")}
    f = {k[7:]: v for k, v in a.items() if k.startswith("L0_ffn_")}

    def chunks(w):
        return [w[:, i:i + P] for i in range(0, w.shape[1], P)]

    wl = []
    for l in range(LAYERS):
        wl += [r[n][l].T for n in ("Wr", "Wk", "Wv", "Wo")] + [r["Wcr"][l].T] + chunks(r["Wck"][l].T)
        wl += [r["Wcv"][l].T[i:i + P] for i in range(0, FF * P, P)]
    wo = np.zeros((2, P, P), np.float32)
    for h in range(HEADS):
        g, place = h % 4, h // 4
        at = 64 * (g % 2) + HEAD * place
        wo[g // 2, at:at + HEAD] = t["Wo"].T[HEAD * h:HEAD * (h + 1)]
    wx = [t[n].T for n in ("Wq", "Wk", "Wv")] + list(wo)
    we = chunks(f["share_Wup"]) + list(f["exp_Wup"]) + [f["share_Wg"]] * SHARED + list(f["exp_Wg"])
    we += [f["share_Wdown"]] * SHARED + list(f["exp_Wdown"])
    vec = [r[n].T for n in ("ln1_w", "ln1_b", "ln2_w", "ln2_b", "time_decay", "time_first", "tmk", "tmv", "tmr",
                            "cmk", "cmr")]
    vec += [f["exp_bup"].T, f["share_bup"].reshape(SHARED, P).T, f["exp_bg"].T, f["share_bg"].reshape(1, P).T]
    rows = np.concatenate([r["ln0_w"], r["ln0_b"], f["norm_w"].ravel(), f["router_b"].ravel(), f["gate_bias"].ravel()])
    bdown = np.concatenate([f["exp_bdown"], f["exp_bdown"], np.stack([f["share_bdown"]] * SHARED)])

    const = np.zeros((P, P + 64), np.float32)
    const[:, :P] = np.eye(P)
    const[:, P:P + 36] = np.tri(EXPERTS, k=-1).reshape(1, 36)
    const[1::2, P + 36] = 1.0
    const[:, P + 38] = 1.0
    for g in range(4):
        const[range(32 * g, 32 * g + GROUPS), range(P + 48, P + 48 + GROUPS)] = -1.0
    for e in range(EXPERTS):
        const[[e, EXPERTS + e], P + 40 + e] = 1.0
    dup = np.zeros((P, 2, 2, GROUPS, P), np.float32)
    for which, highs in enumerate(((0, 2), (0, 1))):
        for g in range(GROUPS):
            for place in range(4):
                for part in range(4):
                    for d in range(HEAD):
                        dup[HEAD * (4 * g + place) + d, which, int(part not in highs), g, 32 * place + 8 * part + d] = 1

    arrays = {
        "xs": np.concatenate([a["x"], a["x"][:STREAMS * ROWS]]),
        "ctxT": a["ctx_1024"].reshape(-1, P).T,
        "biasT": a["fside_BxS2_0"].T,
        "bias_rows": np.broadcast_to(a["fside_BxS2_0"].reshape(1, -1), (P, a["fside_BxS2_0"].size)),
        "wl": np.stack(wl, 1), "wx": np.stack(wx, 1), "we": np.stack(we, 1),
        "wrout": np.concatenate(list(f["router_W"]), 1),
        "vec": np.concatenate(vec, 1), "rows": np.broadcast_to(rows, (P, ROW_N)), "bdown": bdown,
        "const": const, "dup": dup.reshape(P, 2, 2 * GROUPS * P),
    }
    nc = bacc.Bacc("TRN2", target_bir_lowering=False, num_devices=1)
    arrays = {n: np.ascontiguousarray(v) for n, v in arrays.items()}
    args = [nc.dram_tensor(n, v.shape, mb.dt.from_np(v.dtype), kind="ExternalInput").ap() for n, v in arrays.items()]
    out = nc.dram_tensor("out", a["x"].shape, F32, kind="ExternalOutput").ap()
    network(nc, *args, out)
    result = run_bass_kernel_spmd(nc, [arrays], core_ids=[0])
    return result.results[0]["out"]
```
